# Optimizing a Trainium2 kernel written in Bass

```python
import numpy as np
import jax
import jax.numpy as jnp

def _softmax(x, axis=-1):
    return jax.nn.softmax(x, axis=axis)

def _gelu(x):
    return jax.nn.gelu(x, approximate=True)

def _silu(x):
    return jax.nn.silu(x)

def _sigmoid(x):
    return jax.nn.sigmoid(x)

def _layernorm(x, axis=-1, eps=1e-05):
    m = jnp.mean(x, axis=axis, keepdims=True)
    v = jnp.var(x, axis=axis, keepdims=True)
    return (x - m) / jnp.sqrt(v + eps)

def _scatter_add(tgt, idx, src, axis=0):
    return tgt.at[idx].add(src)

def _segment_sum(src, seg, n):
    return jax.ops.segment_sum(src, seg, n)
kernel_name = 'mk_recurrent_d1_jaxref_r2_b293b9'

def setup_inputs(seed: int=0):
    np.random.seed(seed)
    _w = jnp.asarray

    def _L0_attn_setup():
        import jax, jax.numpy as jnp
        import numpy as np
        HIDDEN = 512
        MEM = 128
        DECAY = 0.99

        def _reference_tuple_inner(x, Wq, Wk, Wv, Wo, gate, M0):
            b = x.shape[0]
            q = jnp.einsum('bsh,mh->bsm', x, Wq)
            k = jnp.einsum('bsh,mh->bsm', x, Wk)
            v = jnp.einsum('bsh,mh->bsm', x, Wv)
            qT = jnp.swapaxes(q, 0, 1)
            kT = jnp.swapaxes(k, 0, 1)
            vT = jnp.swapaxes(v, 0, 1)

            def step(M, qkv):
                q_t, k_t, v_t = qkv
                r_t = q_t @ M.T
                outer = v_t.T @ k_t / b
                M_new = DECAY * M + outer
                return (M_new, r_t)
            _, rT = jax.lax.scan(step, M0, (qT, kT, vT))
            retrieved = jnp.swapaxes(rT, 0, 1)
            output = jnp.einsum('bsm,hm->bsh', retrieved, Wo)
            gate_value = jax.nn.sigmoid(gate)
            return (output * gate_value, gate_value)
        key = jax.random.key(seed)
        ks = jax.random.split(key, 6)
        x = jax.random.normal(ks[0], (4, 2048, HIDDEN), dtype=jnp.float32)
        scale = 0.02
        Wq = jax.random.normal(ks[1], (MEM, HIDDEN), dtype=jnp.float32) * scale
        Wk = jax.random.normal(ks[2], (MEM, HIDDEN), dtype=jnp.float32) * scale
        Wv = jax.random.normal(ks[3], (MEM, HIDDEN), dtype=jnp.float32) * scale
        Wo = jax.random.normal(ks[4], (HIDDEN, MEM), dtype=jnp.float32) * scale
        gate = jnp.zeros((1,), dtype=jnp.float32)
        M0 = jnp.zeros((MEM, MEM), dtype=jnp.float32)
        return {'x': x, 'Wq': Wq, 'Wk': Wk, 'Wv': Wv, 'Wo': Wo, 'gate': gate, 'M0': M0}
    _L0_attn_in = _L0_attn_setup()

    def _L0_ffn_setup():
        import jax, jax.numpy as jnp
        import numpy as np
        B, S, H, F, G = (8, 1024, 512, 2048, 128)
        EPS = 1e-05

        def _dequant(q, scales, g):
            K, N = q.shape
            w = (q.astype(jnp.float32) - 128.0).reshape(K // g, g, N) * scales[:, None, :]
            return w.reshape(K, N)
        key = jax.random.key(seed)
        ks = jax.random.split(key, 8)
        x = jax.random.normal(ks[0], (B, S, H), dtype=jnp.float32)
        ln_gamma = jnp.ones((H,), jnp.float32)
        ln_beta = jnp.zeros((H,), jnp.float32)
        fc1_q = jax.random.randint(ks[1], (H, F), 0, 128, dtype=jnp.int32)
        fc2_q = jax.random.randint(ks[2], (F, H), 0, 128, dtype=jnp.int32)
        fc1_scales = jax.random.uniform(ks[3], (H // G, F), jnp.float32) * 0.02 + 0.001
        fc2_scales = jax.random.uniform(ks[4], (F // G, H), jnp.float32) * 0.02 + 0.001
        fc1_bias = jax.random.normal(ks[5], (F,), jnp.float32) * 0.02
        fc2_bias = jax.random.normal(ks[6], (H,), jnp.float32) * 0.02
        return {'x': x, 'ln_gamma': ln_gamma, 'ln_beta': ln_beta, 'fc1_q': fc1_q, 'fc1_scales': fc1_scales, 'fc1_bias': fc1_bias, 'fc2_q': fc2_q, 'fc2_scales': fc2_scales, 'fc2_bias': fc2_bias}
    _L0_ffn_in = _L0_ffn_setup()
    _d = {'L0_attn_x': _L0_attn_in['x'], 'L0_attn_Wq': _L0_attn_in['Wq'], 'L0_attn_Wk': _L0_attn_in['Wk'], 'L0_attn_Wv': _L0_attn_in['Wv'], 'L0_attn_Wo': _L0_attn_in['Wo'], 'L0_attn_gate': _L0_attn_in['gate'], 'L0_attn_M0': _L0_attn_in['M0'], 'L0_ffn_ln_gamma': _L0_ffn_in['ln_gamma'], 'L0_ffn_ln_beta': _L0_ffn_in['ln_beta'], 'L0_ffn_fc1_q': _L0_ffn_in['fc1_q'], 'L0_ffn_fc1_scales': _L0_ffn_in['fc1_scales'], 'L0_ffn_fc1_bias': _L0_ffn_in['fc1_bias'], 'L0_ffn_fc2_q': _L0_ffn_in['fc2_q'], 'L0_ffn_fc2_scales': _L0_ffn_in['fc2_scales'], 'L0_ffn_fc2_bias': _L0_ffn_in['fc2_bias']}
    _x0 = _d['L0_attn_x']
    _d['L0_attn_x'] = jax.random.normal(jax.random.fold_in(jax.random.key(seed), 1), (4, 2048, 512), dtype=_x0.dtype)
    del _x0
    return _d

def reference(L0_attn_x, L0_attn_Wq, L0_attn_Wk, L0_attn_Wv, L0_attn_Wo, L0_attn_gate, L0_attn_M0, L0_ffn_ln_gamma, L0_ffn_ln_beta, L0_ffn_fc1_q, L0_ffn_fc1_scales, L0_ffn_fc1_bias, L0_ffn_fc2_q, L0_ffn_fc2_scales, L0_ffn_fc2_bias):

    def _L0_attn_ref(x, Wq, Wk, Wv, Wo, gate, M0):
        import jax, jax.numpy as jnp
        import numpy as np
        HIDDEN = 512
        MEM = 128
        DECAY = 0.99

        def _reference_tuple_inner(x, Wq, Wk, Wv, Wo, gate, M0):
            b = x.shape[0]
            q = jnp.einsum('bsh,mh->bsm', x, Wq)
            k = jnp.einsum('bsh,mh->bsm', x, Wk)
            v = jnp.einsum('bsh,mh->bsm', x, Wv)
            qT = jnp.swapaxes(q, 0, 1)
            kT = jnp.swapaxes(k, 0, 1)
            vT = jnp.swapaxes(v, 0, 1)

            def step(M, qkv):
                q_t, k_t, v_t = qkv
                r_t = q_t @ M.T
                outer = v_t.T @ k_t / b
                M_new = DECAY * M + outer
                return (M_new, r_t)
            _, rT = jax.lax.scan(step, M0, (qT, kT, vT))
            retrieved = jnp.swapaxes(rT, 0, 1)
            output = jnp.einsum('bsm,hm->bsh', retrieved, Wo)
            gate_value = jax.nn.sigmoid(gate)
            return (output * gate_value, gate_value)
        return _reference_tuple_inner(x, Wq, Wk, Wv, Wo, gate, M0)[0]

    def _L0_ffn_ref(x, ln_gamma, ln_beta, fc1_q, fc1_scales, fc1_bias, fc2_q, fc2_scales, fc2_bias):
        import jax, jax.numpy as jnp
        import numpy as np
        B, S, H, F, G = (8, 1024, 512, 2048, 128)
        EPS = 1e-05

        def _dequant(q, scales, g):
            K, N = q.shape
            w = (q.astype(jnp.float32) - 128.0).reshape(K // g, g, N) * scales[:, None, :]
            return w.reshape(K, N)
        residual = x
        mu = jnp.mean(x, axis=-1, keepdims=True)
        var = jnp.mean(jnp.square(x - mu), axis=-1, keepdims=True)
        h = (x - mu) * jax.lax.rsqrt(var + EPS) * ln_gamma + ln_beta
        hf = h.reshape(-1, H)
        w1 = _dequant(fc1_q, fc1_scales, G)
        y = hf @ w1 + fc1_bias
        y = jax.nn.silu(y)
        w2 = _dequant(fc2_q, fc2_scales, G)
        z = y @ w2 + fc2_bias
        return residual + 0.5 * z.reshape(residual.shape)
    x = L0_attn_x
    xn = _layernorm(x, axis=-1)
    s = _L0_attn_ref(xn, L0_attn_Wq, L0_attn_Wk, L0_attn_Wv, L0_attn_Wo, L0_attn_gate, L0_attn_M0)
    g = _silu(_L0_ffn_ref(xn, L0_ffn_ln_gamma, L0_ffn_ln_beta, L0_ffn_fc1_q, L0_ffn_fc1_scales, L0_ffn_fc1_bias, L0_ffn_fc2_q, L0_ffn_fc2_scales, L0_ffn_fc2_bias))
    x = x + s * g
    return x

_drawn_inputs = setup_inputs


def setup_inputs(seed=0):
    import zlib

    import numpy as np

    out = dict(_drawn_inputs(seed))
    spreads = {'L0_attn_M0': (0.0, 0.1), 'L0_ffn_ln_gamma': (1.0, 0.2), 'L0_ffn_ln_beta': (0.0, 0.1)}
    factors = {}
    for name, (base, spread) in spreads.items():
        noise = np.random.default_rng([zlib.crc32(name.encode()), seed]).standard_normal(out[name].shape)
        drawn = base * np.exp(spread * noise) if base else spread * noise
        out[name] = jnp.asarray(drawn.astype(out[name].dtype))
    for name, factor in factors.items():
        out[name] = (out[name] * factor).astype(out[name].dtype)
    return out
```

```python
from contextlib import ExitStack

import numpy as np

import concourse.bass as bass
from concourse import mybir

F32 = mybir.dt.float32
F16 = mybir.dt.float16
I32 = mybir.dt.int32
ALU = mybir.AluOpType
ACT = mybir.ActivationFunctionType
AX = mybir.AxisListType

P = 128
EPS = 1e-5
DECAY = float(np.float32(0.99))
ZERO_POINT = 128.0
G_SCALE = 1024.0
TOP = 2.0 ** 14
ROW_STEPS = 10
TINY = 1e-30
EXACT_Q = 1920.0

SIDE = {}
for _i in range(4):
    for _n, _job in enumerate(("qkv", "qkt", "scores", "read", "wo")):
        SIDE[12 * _i + 2 * _n] = (_job, _i)
for _k in range(4):
    SIDE[48 + 4 * _k] = ("turn", _k)
SIDE_BANK = {e: n % 2 for n, e in enumerate(sorted(SIDE))}
BEFORE_IN_BANK = {e: sorted(SIDE)[n - 2] for n, e in enumerate(sorted(SIDE))}


def build(nc, x, wqkv, wo, gate, m0, gamma, beta, q1, s1, b1, q2, s2, s2_flat, b2, out):
    B, S, H = x.shape
    M = m0.shape[0]
    F = q1.shape[1]
    KC = H // P
    FB = F // P
    TAU = P // B
    NT = 4
    T = NT * P
    STEPS_T = NT * TAU
    NCH = S // STEPS_T
    QKV = 3 * M
    DECAY_TILE = DECAY ** TAU
    assert KC == NT == 4 and FB == 16 and NCH % 2 == 0 and M == P

    ctx = ExitStack()
    with ctx:
        def sb(name, shape, dt):
            return ctx.enter_context(nc.sbuf_tensor(name, shape, dt))

        def sem(name):
            return ctx.enter_context(nc.semaphore(name))

        q1_sb = sb("q1_sb", [P, KC, 4, 2, T], F16)
        w2_sb = sb("w2_sb", [P, FB, 2, H], F16)
        q1_in_sb = q1_sb[:].rearrange("p g n t c -> p g n (t c)").bitcast(I32)
        q2_in_sb = w2_sb[:].rearrange("p j t h -> p j (t h)").bitcast(I32)
        wqkv_hi = sb("wqkv_hi", [P, KC, QKV], F16)
        wqkv_lo = sb("wqkv_lo", [P, KC, QKV], F16)
        wo_sb = sb("wo_sb", [P, H], F32)
        par = sb("par", [P, 2 * KC + FB + 2 * FB * KC], F32)
        gamma_c = par[:, 0:KC]
        beta_c = par[:, KC:2 * KC]
        b1_c = par[:, 2 * KC:2 * KC + FB]
        s1_c = par[:, 2 * KC + FB:2 * KC + FB + FB * KC]
        s2_c = par[:, 2 * KC + FB + FB * KC:]
        gate_c = sb("gate_c", [P, 2], F32)
        b2_half = sb("b2_half", [P, H], F32)
        quarter_tops = sb("quarter_tops", [P, 4], F32)
        tops = sb("tops", [P, 6], F32)
        all_tops = sb("all_tops", [P, 6], F32)
        w2_tops = sb("w2_tops", [P, 2], F32)
        all_w2_tops = sb("all_w2_tops", [P, 2], F32)
        bound = sb("bound", [P, 5], F32)
        pow2 = sb("pow2", [P, 5], F32)
        up = sb("up", [P, 5], F32)
        up_h, up_wqkv, up_q1, up_y, up_w2 = (up[:, n:n + 1] for n in range(5))
        mix = sb("mix", [P, 4], F32)
        gamma_s = sb("gamma_s", [P, KC], F32)
        beta_s = sb("beta_s", [P, KC], F32)
        s1_s = sb("s1_s", [P, KC * FB], F32)
        q1_shift = sb("q1_shift", [P, 1], F32)
        w2_up = sb("w2_up", [P, 1], F32)
        z_down = sb("z_down", [P, 1], F32)
        slow_q1 = sb("slow_q1", [P, 1], I32)
        tau_i = sb("tau_i", [P, 2], I32)
        tau_c = sb("tau_c", [P, 2], F32)
        tau_row = sb("tau_row", [P, P], I32)
        decay_c = sb("decay_c", [P, 2], F32)
        powers = sb("powers", [P, 3], F32)
        in_c = sb("in_c", [P, 3], F32)
        ident = sb("ident", [P, P], F32)
        mask = sb("mask", [P, P], F32)
        EPS_AT, MINUS_HALF, HALF, G_SCALE_AT, MINUS_ONE = range(5)
        row_const = sb("row_const", [P, 5, NT], F32)
        xt = sb("xt", [P, 2, NT, H], F32)
        g_rows = sb("g_rows", [P, NT, H], F32)
        pre = sb("pre", [P, NT, H], F32)
        s_rows = sb("s_rows", [P, NT, H], F32)
        g_hi = sb("g_hi", [P, KC, T], F16)
        g_lo = sb("g_lo", [P, KC, T], F16)
        h_full = sb("h_full", [P, 2, T], F32)
        h_hi = sb("h_hi", [P, 2, KC, T], F16)
        h_lo = sb("h_lo", [P, 2, KC, T], F16)
        acc = sb("acc", [P, 2, T], F32)
        y_full = sb("y_full", [P, 2, T], F32)
        y_hi = sb("y_hi", [P, 4, T], F16)
        y_lo = sb("y_lo", [P, 4, T], F16)
        qkv = sb("qkv", [P, 2, QKV], F32)
        qk_t = sb("qk_t", [P, 2 * P], F32)
        s_mask = sb("s_mask", [P, P], F32)
        r_t = sb("r_t", [P, P], F32)
        mem_t = sb("mem_t", [P, M], F32)
        fin = sb("fin", [P, 2, H], F32)
        out_sb = sb("out_sb", [P, 2, H], F32)
        wide = sb("wide", [P, 2, T], F32)
        wqkv_in = pre[:].rearrange("p i h -> p (i h)")[:, 0:KC * QKV].rearrange("p (k n) -> p k n", k=KC)
        s2_row = out_sb
        stat6 = sb("stat6", [P, NT, 6], F32)
        mv = sb("mv", [P, 2, NT, 2], F32)
        rs = sb("rs", [P, 2, NT], F32)
        nmr = sb("nmr", [P, 2, NT], F32)
        gs = sb("gs", [P, 2, NT], F32)
        v2 = sb("v2", [P, 4, NT], F32)
        row_c = sb("row_c", [P, 2, 3, NT], F32)

        blk = [ctx.enter_context(nc.psum_tensor(f"blk{n}", [P, T], F32)) for n in range(2)]
        side = [ctx.enter_context(nc.psum_tensor(f"side{n}", [P, T], F32)) for n in range(2)]
        z = [ctx.enter_context(nc.psum_tensor(f"z{n}", [P, H], F32)) for n in range(NT)]

        par_in, wq_in, wo_in, m_in, gate_in, b2_in = (
            sem(n) for n in ("par_in", "wq_in", "wo_in", "m_in", "gate_in", "b2_in"))
        q1_in = [sem(f"q1_in{n}") for n in range(4)]
        q2_in = [sem(f"q2_in{n}") for n in range(4)]
        s2_in = [sem(f"s2_in{n}") for n in range(2)]
        x_in = [sem(f"x_in{n}") for n in range(2)]
        dve_link, pool_link = sem("dve_link"), sem("pool_link")
        gate_done, wo_gated = sem("gate_done"), sem("wo_gated")
        tops_done, all_tops_done = sem("tops_done"), sem("all_tops_done")
        w2_tops_done, all_w2_tops_done = sem("w2_tops_done"), sem("all_w2_tops_done")
        h_scales, s1_scaled, q1_scale, wqkv_split = (
            sem(n) for n in ("h_scales", "s1_scaled", "q1_scale", "wqkv_split"))
        ident_done, tau_made, tau_done, decay_done, in_c_done = (
            sem(n) for n in ("ident_done", "tau_made", "tau_done", "decay_done", "in_c_done"))
        b2_halved = sem("b2_halved")
        slow_known = sem("slow_known")
        q1_wide, q1_hi_done, q1_done = sem("q1_wide"), sem("q1_hi_done"), sem("q1_done")
        w2_quarter, row_c_done = sem("w2_quarter"), sem("row_c_done")
        w2_wide, w2_hi_done, w2_done = sem("w2_wide"), sem("w2_hi_done"), sem("w2_done")
        blk_done = sem("blk_done")
        acc_first = sem("acc_first")
        acc_done = sem("acc_done")
        silu_done = sem("silu_done")
        y_hi_done = sem("y_hi_done")
        y_lo_done = sem("y_lo_done")
        ffn2_done = sem("ffn2_done")
        z_done = sem("z_done")
        fin_done = sem("fin_done")
        fin_silu = sem("fin_silu")
        fin_mul = sem("fin_mul")
        out_done = sem("out_done")
        stored = [sem(f"stored{n}") for n in range(2)]
        bn_done = sem("bn_done")
        mv_done = sem("mv_done")
        rows_step = sem("rows_step")
        rows_done = sem("rows_done")
        g_done = sem("g_done")
        turn_done = sem("turn_done")
        turn_act = sem("turn_act")
        g_lo_done = sem("g_lo_done")
        h_hi_done = sem("h_hi_done")
        h_done = sem("h_done")
        qkv_done = sem("qkv_done")
        qkv_out = sem("qkv_out")
        qkt_done = sem("qkt_done")
        qkt_out = sem("qkt_out")
        scores_done = sem("scores_done")
        masked = sem("masked")
        read_done = sem("read_done")
        r_out = sem("r_out")
        mem_done = sem("mem_done")
        wo_done = sem("wo_done")
        s_out = sem("s_out")
        pre_act = sem("pre_act")
        pre_done = sem("pre_done")

        block = ctx.enter_context(nc.Block())

        def wait(eng, s, count):
            if not (isinstance(count, int) and count <= 0):
                eng.wait_ge(s, count)

        def each_chunk(eng, body):
            body(0, 0, 1, True, False)
            with eng.Fori(0, NCH // 2 - 1) as it:
                body(it * 2 + 1, 1, it + 2, False, False)
                body(it * 2 + 2, 0, it + 2, False, False)
            body(NCH - 1, 1, 0, False, True)

        @block.sync
        def _(sp):
            def load_x(c, parity):
                for b in range(B):
                    sp.dma_start(xt[b * TAU:(b + 1) * TAU, parity, :, :],
                                 x[b, bass.ds(c * STEPS_T, STEPS_T), :].rearrange("(i t) h -> t i h", t=TAU)
                                 ).then_inc(x_in[parity], 16)

            def store(c, i):
                sp.wait_ge(out_done, 4 * c + i + 1)
                for b in range(B):
                    sp.dma_start(out[b, bass.ds(c * STEPS_T + i * TAU, TAU), :],
                                 out_sb[b * TAU:(b + 1) * TAU, i % 2, :]).then_inc(stored[i % 2], 16)

            load_x(0, 0)
            sp.dma_start(wqkv_in, wqkv).then_inc(wq_in, 16)
            for n in range(4):
                sp.dma_start(q1_in_sb[:, :, n, :], q1.rearrange("(g p) (n c) -> n p g c", p=P, n=4)[n]
                             ).then_inc(q1_in[n], 16)
            sp.dma_start(wo_sb[:], wo).then_inc(wo_in, 16)
            sp.dma_start(mem_t[:], m0).then_inc(m_in, 16)
            for n in range(4):
                sp.dma_start(q2_in_sb[:, 4 * n:4 * n + 4, :], q2.rearrange("(n j p) h -> n p j h", n=4, p=P)[n]
                             ).then_inc(q2_in[n], 16)
            load_x(1, 1)
            for j in range(FB):
                if j >= 2:
                    sp.wait_ge(w2_wide, j - 1)
                sp.dma_start(s2_row[:, j % 2, :], s2[j, :].partition_broadcast(P)).then_inc(s2_in[j % 2], 16)

            def body(c, parity, loads, first, last):
                if not first:
                    for i in range(NT):
                        store(c - 1, i)
                    if not last:
                        load_x(c + 1, 1 - parity)

            each_chunk(sp, body)
            for i in range(NT):
                store(NCH - 1, i)
            for n in range(2):
                sp.wait_ge(stored[n], 64 * 2 * NCH)

        @block.tensor
        def _(pe):
            def bank_free(c, e):
                before = BEFORE_IN_BANK[e]
                job, i = SIDE[before]
                c_before = c if before < e else c - 1
                if job == "turn":
                    c_before = c_before + 1
                read, per_job = {"qkv": (qkv_out, 3), "qkt": (qkt_out, 1), "scores": (masked, 1),
                                 "read": (mem_done, 1), "wo": (s_out, 1), "turn": (g_lo_done, 1)}[job]
                pe.wait_ge(read, per_job * (4 * c_before + i + 1))

            def turn(c, k, bank):
                if k == 0:
                    pe.wait_ge(g_done, 4 * c + 4)
                for i in range(NT):
                    mm = pe.transpose(side[bank][:, i * P:(i + 1) * P], g_rows[:, i, k * P:(k + 1) * P], ident[:])
                mm.then_inc(turn_done, 1)

            def run_side(c, e):
                job, i = SIDE[e]
                bank = side[SIDE_BANK[e]]
                bank_free(c, e)
                if job == "turn":
                    turn(c + 1, i, SIDE_BANK[e])
                elif job == "qkv":
                    if i == 0:
                        pe.wait_ge(g_lo_done, 4 * c + 4)
                    rows = slice(i * P, (i + 1) * P)
                    for k in range(KC):
                        for n, (a, w) in enumerate(((g_hi, wqkv_hi), (g_lo, wqkv_hi), (g_hi, wqkv_lo))):
                            mm = pe.matmul(bank[:, 0:QKV], a[:, k, rows], w[:, k, :],
                                           start=(k == 0 and n == 0), stop=(k == KC - 1 and n == 2))
                    mm.then_inc(qkv_done, 1)
                elif job == "qkt":
                    pe.wait_ge(qkv_out, 3 * (4 * c + i + 1))
                    pe.transpose(bank[:, 0:P], qkv[:, i % 2, 0:M], ident[:])
                    pe.transpose(bank[:, P:2 * P], qkv[:, i % 2, M:2 * M], ident[:]).then_inc(qkt_done, 1)
                elif job == "scores":
                    pe.wait_ge(qkt_out, 4 * c + i + 1)
                    pe.matmul(bank[:, 0:P], qk_t[:, P:2 * P], qk_t[:, 0:P], start=True, stop=True
                              ).then_inc(scores_done, 1)
                elif job == "read":
                    pe.wait_ge(masked, 4 * c + i + 1)
                    wait(pe, mem_done, 4 * c + i)
                    pe.matmul(bank[:, 0:P], mem_t[:], qk_t[:, 0:P], start=True, stop=False)
                    pe.matmul(bank[:, 0:P], qkv[:, i % 2, 2 * M:3 * M], s_mask[:], start=False, stop=True)
                    pe.matmul(bank[:, P:2 * P], qkv[:, i % 2, M:2 * M], qkv[:, i % 2, 2 * M:3 * M],
                              start=True, stop=True).then_inc(read_done, 1)
                elif job == "wo":
                    pe.wait_ge(r_out, 4 * c + i + 1)
                    pe.matmul(bank[:], r_t[:], wo_sb[:], start=True, stop=True).then_inc(wo_done, 1)

            def ffn1(c, parity, j, g, slow, first):
                e = 4 * j + g
                if g == 2:
                    pe.wait_ge(acc_first, 16 * c + j + 1)
                elif g == 3:
                    pe.wait_ge(acc_done, 48 * c + 3 * j + 1)
                else:
                    wait(pe, acc_done, 48 * c + 3 * (j - 1) + 2 + g)
                if j == 0:
                    pe.wait_ge(h_done, 4 * c + g + 1)
                if first:
                    pe.wait_ge(q1_done, 4 * (j // 4) + g + 1)
                terms = [(0, h_hi), (0, h_lo)] + ([(1, h_hi)] if slow else [])
                for n, (w, a) in enumerate(terms):
                    mm = pe.matmul(blk[e % 2][:], q1_sb[:, g, j // 4, w, j % 4 * P:(j % 4 + 1) * P], a[:, parity, g, :],
                                   start=(n == 0), stop=(n == len(terms) - 1))
                mm.then_inc(blk_done, 1)

            def ffn2(c, j, i, first):
                if i == 0:
                    pe.wait_ge(y_lo_done, 16 * c + j + 1)
                    if first:
                        pe.wait_ge(w2_done, j + 1)
                if j == 0:
                    wait(pe, fin_done, 4 * (c - 1) + i + 1)
                rows = slice(i * P, (i + 1) * P)
                for n, (a, w) in enumerate(((y_hi, 0), (y_lo, 0), (y_hi, 1))):
                    mm = pe.matmul(z[i][:], a[:, j % 4, rows], w2_sb[:, j, w, :],
                                   start=(j == 0 and n == 0), stop=(j == FB - 1 and n == 2))
                if j == FB - 1:
                    mm.then_inc(z_done, 1)
                elif i == NT - 1:
                    mm.then_inc(ffn2_done, 1)

            def all_chunks(slow):
                def body(c, parity, loads, first, last):
                    for j in range(FB):
                        for g in range(KC):
                            e = 4 * j + g
                            ffn1(c, parity, j, g, slow, first)
                            if j >= 2:
                                ffn2(c, j - 2, g, first)
                            elif not first:
                                ffn2(c - 1, j + FB - 2, g, False)
                            if e in SIDE and not (last and SIDE[e][0] == "turn"):
                                run_side(c, e)
                each_chunk(pe, body)
                for j in (FB - 2, FB - 1):
                    for i in range(NT):
                        ffn2(NCH - 1, j, i, False)

            pe.wait_ge(ident_done, 2)
            for k in range(KC):
                if k >= 2:
                    pe.wait_ge(g_lo_done, k - 1)
                turn(0, k, k % 2)
            pe.wait_ge(wqkv_split, 1)
            pe.wait_ge(wo_gated, 1)
            pe.wait_ge(m_in, 16)
            pe.wait_ge(slow_known, 1)
            slow = pe.value_load(slow_q1[0:1, 0:1], min_val=0, max_val=1)
            with pe.If(slow > 0):
                all_chunks(True)
            with pe.Else():
                all_chunks(False)

        @block.scalar
        def _(act):
            for n, src in enumerate((gamma, beta, b1, s1, s2_flat)):
                act.dma_start((gamma_c, beta_c, b1_c, s1_c, s2_c)[n], src).then_inc(par_in, 16)
            act.dma_start(gate_c[:, 0:1], gate.partition_broadcast(P)).then_inc(gate_in, 16)
            act.dma_start(b2_half[:], b2.partition_broadcast(P)).then_inc(b2_in, 16)
            act.wait_ge(gate_in, 16)
            act.activation(gate_c[:, 1:2], gate_c[:, 0:1], ACT.Sigmoid).then_inc(gate_done, 1)

            def turned(c, k, bank):
                act.wait_ge(turn_done, 4 * c + k + 1)
                wait(act, qkv_done, 4 * c)
                act.activation(g_hi[:, k, :], side[bank][:], ACT.Copy).then_inc(turn_act, 1)
                wait(act, h_done, 4 * c + k - 1)
                act.activation(h_full[:, k % 2, :], side[bank][:], ACT.Identity,
                               bias=beta_s[:, k:k + 1], scale=gamma_s[:, k:k + 1]).then_inc(turn_act, 1)

            def side_out(c, parity, e):
                job, i = SIDE[e]
                bank = side[SIDE_BANK[e]]
                if job == "turn":
                    turned(c + 1, i, SIDE_BANK[e])
                elif job == "qkv":
                    act.wait_ge(qkv_done, 4 * c + i + 1)
                    act.wait_ge(row_c_done, c + 1)
                    wait(act, read_done, 4 * c + i - 1)
                    for n in range(3):
                        act.activation(qkv[:, i % 2, n * M:(n + 1) * M], bank[:, n * M:(n + 1) * M], ACT.Copy,
                                       scale=row_c[:, parity, n, i:i + 1]).then_inc(qkv_out, 1)
                elif job == "qkt":
                    act.wait_ge(qkt_done, 4 * c + i + 1)
                    wait(act, read_done, 4 * c + i)
                    act.activation(qk_t[:], bank[:, 0:2 * P], ACT.Copy).then_inc(qkt_out, 1)
                elif job == "read":
                    act.wait_ge(read_done, 4 * c + i + 1)
                    wait(act, wo_done, 4 * c + i)
                    act.activation(r_t[:], bank[:, 0:P], ACT.Copy).then_inc(r_out, 1)
                elif job == "wo":
                    act.wait_ge(wo_done, 4 * c + i + 1)
                    wait(act, fin_mul, 4 * (c - 1) + i + 1)
                    act.activation(s_rows[:, i, :], bank[:], ACT.Copy).then_inc(s_out, 1)

            def first_block(c, j):
                act.wait_ge(blk_done, 64 * c + 4 * j + 1)
                wait(act, silu_done, 16 * c + j - 1)
                act.activation(acc[:, j % 2, :], blk[0][:], ACT.Identity, bias=b1_c[:, j:j + 1],
                               scale=s1_s[:, j:j + 1]).then_inc(acc_first, 1)

            def silu(c, j):
                act.wait_ge(acc_done, 48 * c + 3 * j + 3)
                wait(act, y_lo_done, 16 * c + j - 1)
                act.activation(y_full[:, j % 2, :], acc[:, j % 2, :], ACT.Silu).then_inc(silu_done, 1)
                act.wait_ge(silu_done, 16 * c + j + 1)
                if j >= 4:
                    act.wait_ge(ffn2_done, 15 * c + j - 3)
                elif j == 3:
                    wait(act, z_done, 4 * c)
                else:
                    wait(act, ffn2_done, 15 * (c - 1) + j + FB - 3)
                act.activation(y_hi[:, j % 4, :], y_full[:, j % 2, :], ACT.Copy, scale=up_y
                               ).then_inc(y_hi_done, 1)

            def gate_silu(c, i):
                act.wait_ge(fin_done, 4 * c + i + 1)
                act.activation(fin[:, i % 2, :], fin[:, i % 2, :], ACT.Silu).then_inc(fin_silu, 1)

            def xn(c, parity, i):
                wait(act, fin_done, 4 * (c - 1) + i + 1)
                act.activation(pre[:, i, :], xt[:, parity, i, :], ACT.Identity, bias=nmr[:, parity, i:i + 1],
                               scale=rs[:, parity, i:i + 1]).then_inc(pre_act, 1)

            def body(c, parity, loads, first, last):
                for j in range(FB):
                    for g in range(KC):
                        e = 4 * j + g
                        if g == 0:
                            first_block(c, j)
                        if e - 1 in SIDE and SIDE[e - 1][0] != "scores" and not (last and SIDE[e - 1][0] == "turn"):
                            side_out(c, parity, e - 1)
                        if g == 1 and j >= 1:
                            silu(c, j - 1)
                        elif g == 1 and not first:
                            silu(c - 1, FB - 1)
                        if not first and 6 <= e < 6 + NT:
                            gate_silu(c - 1, e - 6)
                        if 16 <= e < 16 + 2 * NT and e % 2 == 0:
                            xn(c, parity, (e - 16) // 2)

            act.wait_ge(h_scales, 1)
            for k in range(KC):
                turned(0, k, k % 2)
            act.wait_ge(q1_scale, 1)
            for n in range(FB):
                if n >= 2:
                    act.wait_ge(q1_done, n - 1)
                act.activation(wide[:, n % 2, :], q1_in_sb[:, n % 4, n // 4, :], ACT.Identity,
                               bias=q1_shift[:, 0:1], scale=up_q1).then_inc(q1_wide, 1)
            act.wait_ge(wo_in, 16)
            act.wait_ge(gate_done, 1)
            act.activation(wo_sb[:], wo_sb[:], ACT.Copy, scale=gate_c[:, 1:2]).then_inc(wo_gated, 1)
            act.wait_ge(s1_scaled, 1)
            each_chunk(act, body)
            silu(NCH - 1, FB - 1)
            for i in range(NT):
                gate_silu(NCH - 1, i)

        @block.vector
        def _(dve):
            def stats(c, parity, i, loads):
                if i == 0:
                    dve.wait_ge(x_in[parity], 64 * loads)
                dve.bn_stats(stat6[:, i, :], xt[:, parity, i, :]).then_inc(bn_done, 1)

            def moments(c, parity, i):
                dve.bn_aggr(mv[:, parity, i, :], stat6[:, i, :]).then_inc(mv_done, 1)

            def normalise(c, parity, i):
                if i == 0:
                    dve.wait_ge(rows_done, c + 1)
                    wait(dve, turn_done, 4 * c)
                dve.tensor_scalar(g_rows[:, i, :], xt[:, parity, i, :], mv[:, parity, i, 0:1],
                                  gs[:, parity, i:i + 1], ALU.subtract, ALU.mult).then_inc(g_done, 1)

            def turned_low(c, parity, k, bank):
                dve.wait_ge(turn_act, 2 * (4 * c + k + 1))
                dve.tensor_tensor(g_lo[:, k, :], side[bank][:], g_hi[:, k, :], ALU.subtract
                                  ).then_inc(g_lo_done, 1)
                if k == 0:
                    wait(dve, blk_done, 64 * (c - 1))
                dve.tensor_copy(h_hi[:, parity, k, :], h_full[:, k % 2, :]).then_inc(h_hi_done, 1)

            def side_out(c, parity, e):
                job, i = SIDE[e]
                bank = side[SIDE_BANK[e]]
                if job == "turn":
                    turned_low(c + 1, 1 - parity, i, SIDE_BANK[e])
                elif job == "scores":
                    dve.wait_ge(scores_done, 4 * c + i + 1)
                    wait(dve, read_done, 4 * c + i)
                    dve.tensor_tensor(s_mask[:], bank[:, 0:P], mask[:], ALU.mult).then_inc(masked, 1)
                elif job == "read":
                    dve.wait_ge(r_out, 4 * c + i + 1)
                    wait(dve, mem_done, 4 * c + i)
                    dve.scalar_tensor_tensor(mem_t[:], mem_t[:], DECAY_TILE, bank[:, P:2 * P], ALU.mult, ALU.add
                                             ).then_inc(mem_done, 1)

            def add_block(c, j, g):
                dve.wait_ge(blk_done, 64 * c + 4 * j + g + 1)
                if g == 1:
                    dve.wait_ge(acc_first, 16 * c + j + 1)
                else:
                    dve.wait_ge(acc_done, 48 * c + 3 * j + g - 1)
                dve.scalar_tensor_tensor(acc[:, j % 2, :], blk[g % 2][:], s1_s[:, g * FB + j:g * FB + j + 1],
                                         acc[:, j % 2, :], ALU.mult, ALU.add).then_inc(acc_done, 1)

            def y_low(c, j):
                dve.wait_ge(y_hi_done, 16 * c + j + 1)
                dve.scalar_tensor_tensor(y_lo[:, j % 4, :], y_full[:, j % 2, :], up_y, y_hi[:, j % 4, :],
                                         ALU.mult, ALU.subtract).then_inc(y_lo_done, 1)

            def finish(c, i, last=False):
                dve.wait_ge(z_done, 4 * c + i + 1)
                dve.wait_ge(pre_done, 4 * c + i + 1)
                if i >= 2 or last:
                    dve.wait_ge(out_done, 4 * c + i - 1)
                dve.scalar_tensor_tensor(fin[:, i % 2, :], z[i][:], z_down[:, 0:1], pre[:, i, :],
                                         ALU.mult, ALU.add).then_inc(fin_done, 1)

            def w2_top(n):
                dve.wait_ge(q2_in[n], 16)
                dve.tensor_reduce(quarter_tops[:, n:n + 1], q2_in_sb[:, 4 * n:4 * n + 4, :], AX.XY, ALU.max,
                                  apply_absolute_value=True).then_inc(w2_quarter, 1)

            def w2_all_tops():
                dve.wait_ge(w2_quarter, 4)
                dve.tensor_reduce(w2_tops[:, 0:1], quarter_tops[:], AX.X, ALU.max)
                dve.tensor_reduce(w2_tops[:, 1:2], s2_c, AX.X, ALU.max, apply_absolute_value=True
                                  ).then_inc(w2_tops_done, 1)

            def w2_scale():
                dve.wait_ge(all_w2_tops_done, 1)
                link(dve.tensor_scalar(mix[:, 0:1], all_w2_tops[:, 0:1], ZERO_POINT, 0.5, ALU.add, ALU.mult))
                link(dve.tensor_scalar(bound[:, 4:5], mix[:, 0:1], all_w2_tops[:, 1:2], TINY, ALU.mult, ALU.max))
                power_of_two(slice(4, 5))
                link(dve.tensor_scalar(w2_up[:], up_w2, 0.5, None, ALU.mult))
                link(dve.tensor_scalar(z_down[:], pow2[:, 4:5], pow2[:, 3:4], 1.0 / (TOP * TOP), ALU.mult, ALU.mult))

            def w2_parts(j):
                dve.wait_ge(s2_in[j % 2], 16 * (j // 2 + 1))
                dve.scalar_tensor_tensor(wide[:, 0, :], q2_in_sb[:, j, :], -ZERO_POINT, s2_row[:, j % 2, :],
                                         ALU.add, ALU.mult).then_inc(w2_wide, 1)
                dve.wait_ge(w2_wide, j + 1)
                dve.tensor_scalar(w2_sb[:, j, 0, :], wide[:, 0, :], w2_up[:, 0:1], None, ALU.mult
                                  ).then_inc(w2_hi_done, 1)
                dve.wait_ge(w2_hi_done, j + 1)
                dve.scalar_tensor_tensor(w2_sb[:, j, 1, :], wide[:, 0, :], w2_up[:, 0:1], w2_sb[:, j, 0, :],
                                         ALU.mult, ALU.subtract).then_inc(w2_done, 1)

            def body(c, parity, loads, first, last):
                for j in range(FB):
                    for g in range(KC):
                        e = 4 * j + g
                        if not last and e == 33:
                            dve.wait_ge(bn_done, 4 * (c + 1) + NT)
                        if g >= 1:
                            add_block(c, j, g)
                        if e - 1 in SIDE and SIDE[e - 1][0] in ("turn", "scores", "read") \
                                and not (last and SIDE[e - 1][0] == "turn"):
                            side_out(c, parity, e - 1)
                        if g == 2 and j >= 1:
                            y_low(c, j - 1)
                        elif g == 2 and not first:
                            y_low(c - 1, FB - 1)
                        if not first and 5 <= e < 5 + NT:
                            finish(c - 1, e - 5)
                        if first and e < 4:
                            w2_top(e)
                        if first and e == 3:
                            w2_all_tops()
                        if first and e == 5:
                            w2_scale()
                        if first and e >= 5 and (e - 5) % 3 == 0 and (e - 5) // 3 < FB:
                            w2_parts((e - 5) // 3)
                        if not last:
                            if e in (24, 26, 28, 30):
                                stats(c + 1, 1 - parity, (e - 24) // 2, loads)
                            if e in (33, 34):
                                moments(c + 1, 1 - parity, 2 * (e - 33))
                                moments(c + 1, 1 - parity, 2 * (e - 33) + 1)
                            if e in (42, 43, 44, 45):
                                normalise(c + 1, 1 - parity, e - 42)

            links = [0]

            def link(ins):
                links[0] += 1
                ins.then_inc(dve_link, 1)
                dve.wait_ge(dve_link, links[0])

            def power_of_two(n):
                link(dve.tensor_scalar(pow2[:, n].bitcast(I32), bound[:, n].bitcast(I32), 0x7F800000, None,
                                       ALU.bitwise_and))
                link(dve.reciprocal(up[:, n], pow2[:, n]))
                link(dve.tensor_scalar(up[:, n], up[:, n], TOP, None, ALU.mult))

            def top(n, src, axis=AX.X):
                return dve.tensor_reduce(tops[:, n:n + 1], src, axis, ALU.max, apply_absolute_value=True)

            for i in range(NT):
                stats(0, 0, i, 1)
            dve.wait_ge(bn_done, NT)
            for i in range(NT):
                moments(0, 0, i)
            dve.wait_ge(par_in, 16 * 5)
            top(0, gamma_c)
            top(1, beta_c)
            top(2, s1_c)
            top(3, b1_c)
            dve.wait_ge(wq_in, 16)
            top(4, wqkv_in, AX.XY)
            for i in range(NT):
                normalise(0, 0, i)
            for n in range(4):
                dve.wait_ge(q1_in[n], 16)
                last = dve.tensor_reduce(quarter_tops[:, n:n + 1], q1_in_sb[:, :, n, :], AX.XY, ALU.max,
                                         apply_absolute_value=True)
            link(last)
            top(5, quarter_tops[:]).then_inc(tops_done, 1)
            dve.wait_ge(all_tops_done, 1)
            top_gamma, top_beta, top_s1, top_b1, top_wqkv, top_q1 = (all_tops[:, n:n + 1] for n in range(6))
            link(dve.scalar_tensor_tensor(bound[:, 0:1], top_gamma, float(H) ** 0.5, top_beta, ALU.mult, ALU.add))
            link(dve.tensor_copy(bound[:, 1:2], top_wqkv))
            link(dve.tensor_scalar(bound[:, 2:3], top_q1, ZERO_POINT, None, ALU.add))
            link(dve.tensor_scalar(mix[:, 0:1], top_gamma, top_beta, float(H), ALU.add, ALU.mult))
            link(dve.tensor_tensor(mix[:, 1:2], mix[:, 0:1], bound[:, 2:3], ALU.mult))
            link(dve.tensor_scalar(bound[:, 3:4], mix[:, 1:2], top_s1, top_b1, ALU.mult, ALU.add))
            link(dve.tensor_scalar(bound[:, 0:4], bound[:, 0:4], TINY, None, ALU.max))
            power_of_two(slice(0, 4))
            dve.tensor_scalar(gamma_s[:], gamma_c, up_h, 1.0 / G_SCALE, ALU.mult, ALU.mult)
            dve.tensor_scalar(beta_s[:], beta_c, up_h, None, ALU.mult).then_inc(h_scales, 1)
            dve.tensor_scalar(q1_shift[:], up_q1, -ZERO_POINT, None, ALU.mult).then_inc(q1_scale, 1)
            link(dve.tensor_scalar(slow_q1[:], top_q1, EXACT_Q, None, ALU.is_gt))
            dve.engine_nop().then_inc(slow_known, 1)
            for k in range(KC):
                turned_low(0, 0, k, k % 2)
            link(dve.tensor_tensor(mix[:, 2:3], pow2[:, 0:1], pow2[:, 2:3], ALU.mult))
            dve.tensor_scalar(s1_s[:], s1_c, mix[:, 2:3], 1.0 / (TOP * TOP), ALU.mult, ALU.mult).then_inc(s1_scaled, 1)

            def q1_parts(slow):
                for n in range(FB):
                    g, quarter = n % 4, n // 4
                    dve.wait_ge(q1_wide, n + 1)
                    ins = dve.tensor_copy(q1_sb[:, g, quarter, 0, :], wide[:, n % 2, :])
                    if slow:
                        ins.then_inc(q1_hi_done, 1)
                        dve.wait_ge(q1_hi_done, n + 1)
                        ins = dve.tensor_tensor(q1_sb[:, g, quarter, 1, :], wide[:, n % 2, :],
                                                q1_sb[:, g, quarter, 0, :], ALU.subtract)
                    ins.then_inc(q1_done, 1)

            slow = dve.value_load(slow_q1[0:1, 0:1], min_val=0, max_val=1)
            with dve.If(slow > 0):
                q1_parts(True)
            with dve.Else():
                q1_parts(False)
            link(dve.tensor_scalar(wqkv_hi[:], wqkv_in, up_wqkv, None, ALU.mult))
            dve.scalar_tensor_tensor(wqkv_lo[:].rearrange("p k n -> p (k n)"), wqkv_in.rearrange("p k n -> p (k n)"),
                                     up_wqkv, wqkv_hi[:].rearrange("p k n -> p (k n)"), ALU.mult, ALU.subtract
                                     ).then_inc(wqkv_split, 1)
            dve.wait_ge(tau_made, 2)
            link(dve.tensor_scalar(tau_i[:, 1:2], tau_i[:, 0:1], TAU - 1, None, ALU.bitwise_and))
            link(dve.tensor_copy(tau_c[:, 0:1], tau_i[:, 1:2]))
            link(dve.tensor_scalar(tau_c[:, 1:2], tau_c[:, 0:1], -1.0, float(TAU - 1), ALU.mult, ALU.add))
            dve.tensor_scalar(mask[:], tau_row[:], tau_c[:, 0:1], 1.0 / DECAY_TILE, ALU.is_gt, ALU.mult
                              ).then_inc(tau_done, 1)
            dve.wait_ge(decay_done, 1)
            link(dve.tensor_scalar(mix[:, 3:4], pow2[:, 1:2], 1.0 / (TOP * G_SCALE), None, ALU.mult))
            dve.tensor_tensor(in_c[:, 0:1], powers[:, 0:1], mix[:, 3:4], ALU.mult)
            dve.tensor_scalar(in_c[:, 1:2], powers[:, 1:2], mix[:, 3:4], 1.0 / B, ALU.mult, ALU.mult)
            dve.tensor_copy(in_c[:, 2:3], mix[:, 3:4]).then_inc(in_c_done, 1)
            each_chunk(dve, body)
            y_low(NCH - 1, FB - 1)
            for i in range(NT):
                finish(NCH - 1, i, last=True)

        @block.gpsimd
        def _(pool):
            links = [0]

            def link(ins):
                links[0] += 1
                ins.then_inc(pool_link, 1)
                pool.wait_ge(pool_link, links[0])

            def rows(c, parity):
                pool.wait_ge(mv_done, 4 * c + 4)
                mean, var = mv[:, parity, :, 0], mv[:, parity, :, 1]
                t = [v2[:, n, :] for n in range(4)]
                count = [ROW_STEPS * c]

                def step(ins):
                    count[0] = count[0] + 1
                    ins.then_inc(rows_step, 1)
                    pool.wait_ge(rows_step, count[0])

                step(pool.tensor_tensor(t[0], var, row_const[:, EPS_AT, :], ALU.add))
                step(pool.tensor_tensor(rs[:, parity, :], t[0], row_const[:, MINUS_HALF, :], ALU.pow))
                step(pool.tensor_tensor(t[1], var, rs[:, parity, :], ALU.mult))
                step(pool.tensor_tensor(t[2], t[1], rs[:, parity, :], ALU.mult))
                step(pool.tensor_tensor(t[3], t[2], row_const[:, EPS_AT, :], ALU.add))
                step(pool.tensor_tensor(t[0], t[3], row_const[:, MINUS_HALF, :], ALU.pow))
                step(pool.tensor_tensor(t[1], t[3], row_const[:, HALF, :], ALU.pow))
                step(pool.tensor_tensor(t[2], t[0], rs[:, parity, :], ALU.mult))
                step(pool.tensor_tensor(gs[:, parity, :], t[2], row_const[:, G_SCALE_AT, :], ALU.mult))
                step(pool.tensor_tensor(t[3], mean, rs[:, parity, :], ALU.mult))
                pool.tensor_tensor(nmr[:, parity, :], t[3], row_const[:, MINUS_ONE, :], ALU.mult
                                   ).then_inc(rows_done, 1)

            def row_scales(c, parity):
                if isinstance(c, int) and c == 0:
                    pool.wait_ge(in_c_done, 1)
                for n in range(3):
                    last = pool.tensor_tensor(row_c[:, parity, n, :], v2[:, 1, :],
                                              in_c[:, n:n + 1].to_broadcast([P, NT]), ALU.mult)
                last.then_inc(row_c_done, 1)

            def h_low(c, parity, k):
                pool.wait_ge(h_hi_done, 4 * c + k + 1)
                pool.tensor_tensor(h_lo[:, parity, k, :], h_full[:, k % 2, :], h_hi[:, parity, k, :], ALU.subtract
                                   ).then_inc(h_done, 1)

            def add_b2(c, i):
                pool.wait_ge(pre_act, 4 * c + i + 1)
                pool.tensor_tensor(pre[:, i, :], pre[:, i, :], b2_half[:], ALU.add).then_inc(pre_done, 1)

            def output(c, parity, i):
                pool.wait_ge(fin_silu, 4 * c + i + 1)
                pool.wait_ge(s_out, 4 * c + i + 1)
                pool.tensor_tensor(fin[:, i % 2, :], fin[:, i % 2, :], s_rows[:, i, :], ALU.mult
                                   ).then_inc(fin_mul, 1)
                pool.wait_ge(fin_mul, 4 * c + i + 1)
                wait(pool, stored[i % 2], 64 * (2 * c + i // 2))
                pool.tensor_tensor(out_sb[:, i % 2, :], fin[:, i % 2, :], xt[:, parity, i, :], ALU.add
                                   ).then_inc(out_done, 1)

            def body(c, parity, loads, first, last):
                for e in range(64):
                    if not first and 7 <= e < 7 + NT:
                        output(c - 1, 1 - parity, e - 7)
                    if 17 <= e < 17 + 2 * NT and e % 2 == 1:
                        add_b2(c, (e - 17) // 2)
                    if not last and e == 36:
                        rows(c + 1, 1 - parity)
                        row_scales(c + 1, 1 - parity)
                    if not last and e - 2 in SIDE and SIDE[e - 2][0] == "turn":
                        h_low(c + 1, 1 - parity, SIDE[e - 2][1])

            link(pool.memset(ident[:], 0.0))
            pool.affine_select(out=ident[:], in_=ident[:], compare_op=ALU.not_equal, fill=1.0, base=0,
                               pattern=[[-1, P]], channel_multiplier=1).then_inc(ident_done, 2)
            for at, value in ((EPS_AT, EPS), (MINUS_HALF, -0.5), (HALF, 0.5), (G_SCALE_AT, G_SCALE),
                              (MINUS_ONE, -1.0)):
                pool.memset(row_const[:, at, :], value)
            pool.memset(decay_c[:], DECAY)
            pool.iota(tau_i[:, 0:1], [[1, 1]], base=0, channel_multiplier=1).then_inc(tau_made, 1)
            pool.iota(tau_row[:], [[0, B], [1, TAU]], base=0, channel_multiplier=0).then_inc(tau_made, 1)
            pool.wait_ge(tau_made, 2)
            rows(0, 0)
            pool.wait_ge(tops_done, 1)
            pool.partition_all_reduce(all_tops[:], tops[:], P, bass.bass_isa.ReduceOp.max).then_inc(all_tops_done, 1)
            for k in range(KC):
                h_low(0, 0, k)
            pool.wait_ge(tau_done, 1)
            pool.tensor_tensor(powers[:, 0:2], decay_c[:], tau_c[:], ALU.pow).then_inc(decay_done, 1)
            row_scales(0, 0)
            pool.wait_ge(b2_in, 16)
            link(pool.tensor_scalar(b2_half[:], b2_half[:], 0.5, None, ALU.mult))
            pool.wait_ge(w2_tops_done, 1)
            pool.partition_all_reduce(all_w2_tops[:], w2_tops[:], P, bass.bass_isa.ReduceOp.max
                                      ).then_inc(all_w2_tops_done, 1)
            each_chunk(pool, body)
            for i in range(NT):
                output(NCH - 1, 1, i)


_INS = ["x", "wqkv", "wo", "gate", "m0", "gamma", "beta", "q1", "s1", "b1", "q2", "s2", "s2_flat", "b2"]


def kernel(L0_attn_x, L0_attn_Wq, L0_attn_Wk, L0_attn_Wv, L0_attn_Wo, L0_attn_gate, L0_attn_M0,
           L0_ffn_ln_gamma, L0_ffn_ln_beta, L0_ffn_fc1_q, L0_ffn_fc1_scales, L0_ffn_fc1_bias,
           L0_ffn_fc2_q, L0_ffn_fc2_scales, L0_ffn_fc2_bias):
    import concourse.bacc as bacc
    from concourse.bass_utils import run_bass_kernel_spmd

    def blocks(v):
        return np.asarray(v).reshape(-1, P).T

    wq, wk, wv = (np.asarray(w).T.reshape(-1, P, w.shape[0]).transpose(1, 0, 2)
                  for w in (L0_attn_Wq, L0_attn_Wk, L0_attn_Wv))
    s1 = np.asarray(L0_ffn_fc1_scales)
    values = {
        "x": L0_attn_x, "wqkv": np.concatenate([wq, wk, wv], axis=2), "wo": np.asarray(L0_attn_Wo).T,
        "gate": L0_attn_gate, "m0": np.asarray(L0_attn_M0).T, "gamma": blocks(L0_ffn_ln_gamma),
        "beta": blocks(L0_ffn_ln_beta), "q1": L0_ffn_fc1_q,
        "s1": s1.reshape(s1.shape[0], -1, P).transpose(2, 0, 1).reshape(P, -1),
        "b1": blocks(L0_ffn_fc1_bias), "q2": L0_ffn_fc2_q, "s2": L0_ffn_fc2_scales,
        "s2_flat": np.asarray(L0_ffn_fc2_scales).reshape(P, -1), "b2": L0_ffn_fc2_bias,
    }
    nc = bacc.Bacc("TRN2", target_bir_lowering=False, num_devices=1)
    arrays, args = {}, []
    for name in _INS:
        a = np.ascontiguousarray(values[name])
        arrays[f"in_{name}"] = a
        args.append(nc.dram_tensor(f"in_{name}", a.shape, mybir.dt.from_np(a.dtype), kind="ExternalInput").ap())
    out = nc.dram_tensor("out", L0_attn_x.shape, F32, kind="ExternalOutput").ap()
    build(nc, *args, out)
    return run_bass_kernel_spmd(nc, [arrays], core_ids=[0]).results[0]["out"]
```

```python
from contextlib import ExitStack

import numpy as np

import concourse.bass as bass
from concourse import mybir

F32 = mybir.dt.float32
F16 = mybir.dt.float16
I32 = mybir.dt.int32
ALU = mybir.AluOpType
ACT = mybir.ActivationFunctionType
AX = mybir.AxisListType

P = 128
EPS = 1e-5
DECAY = float(np.float32(0.99))
ZERO_POINT = 128.0
G_SCALE = 1024.0
TOP = 2.0 ** 14
ROW_STEPS = 10
TINY = 1e-30
EXACT_Q = 1920.0

STEPS = 64
PRE = 4
FC2_LAG = 5
Y_RING = 8

FIRST, MIDDLE, LAST, TAIL = range(4)

TAIL_POSITION = 16 - FC2_LAG
FIRST_STEPS = 4 * (FC2_LAG + PRE)

TILE_AT, JOB_AT = (0, 12, 24, 36), (0, 3, 5, 8, 10)
TURN_AT = (43, 49, 54, 59)
TURN_Z_AT = (23, 26, 30, 35)
STATS_AT, MOMENTS_AT, ROWS_AT, NORMALISE_AT = (18, 21, 22, 24), (25, 26), 28, (34, 36, 38, 40)
FIN_LAG, OUT_LAG = 2, 3
TURN_LAG, HLOW_LAG, READ_LAG = 2, 3, 1
PART_LAG = 2
SILU_G, YLOW_G = 1, 2
W2_SCALE_AT, W2_AT, TOP_Q2_AT, Q2_SCALE_AT = 8, (6, 9, 12, 15), (14, 17, 21), 27
Q2_AT = tuple(29 + 5 * n // 2 for n in range(16 - PRE))

SIDE = {}
for _i in range(4):
    for _n, _job in enumerate(("qkv", "qkt", "scores", "read", "wo")):
        SIDE[TILE_AT[_i] + JOB_AT[_n]] = (_job, _i)
    SIDE[TURN_AT[_i]] = ("turn", _i)
    SIDE[TURN_Z_AT[_i]] = ("turn_z", _i)
SIDE_BANK = {e: n % 2 for n, e in enumerate(sorted(SIDE))}
STEP_OF = {v: k for k, v in SIDE.items()}


def has_job(kind, e):
    if e not in SIDE:
        return False
    return {"turn": kind in (FIRST, MIDDLE), "turn_z": kind != FIRST}.get(SIDE[e][0], kind != TAIL)


def job_before(kind, e):
    here = [s for s in sorted(SIDE) if s < e and has_job(kind, s) and SIDE_BANK[s] == SIDE_BANK[e]]
    if here:
        return SIDE[here[-1]], 0
    before = LAST if kind == TAIL else MIDDLE
    return SIDE[[s for s in sorted(SIDE) if has_job(before, s) and SIDE_BANK[s] == SIDE_BANK[e]][-1]], 1


BANKS = 3
FC1_BLOCKS = STEPS
FC2_BLOCKS = 4 + (16 - PRE) * 4


def bank_of(block, blocks):
    return 1 if block == blocks - 1 and block % BANKS == 0 else block % BANKS


def block_before(block, blocks):
    for chunks, blocks_before in ((0, range(block)), (1, range(blocks))):
        same = [n for n in blocks_before if bank_of(n, blocks) == bank_of(block, blocks)]
        if same:
            return same[-1], chunks


def fc2_block(position, g):
    return (4 * position + g) // PRE if position < PRE else 4 + (position - PRE) * 4 + g


def before_of(position, g):
    return divmod(4 * position + g, PRE)


def fc2_at(kind, e):
    chunk = 0
    if e < 0:
        chunk, e = -1, e + STEPS
    position = e // 4 - FC2_LAG
    if position < 0:
        chunk, position = chunk - 1, position + 16
    if (kind == FIRST and chunk < 0) or (kind == TAIL and chunk == 0):
        return None
    return chunk, position, e % 4


def build(nc, x, wqkv, wo, gate, m0, q1, q2, s2, params, out):
    B, S, H = x.shape
    M = m0.shape[0]
    F = q1.shape[1]
    KC = H // P
    FB = F // P
    TAU = P // B
    NT = 4
    T = NT * P
    STEPS_T = NT * TAU
    NCH = S // STEPS_T
    QKV = 3 * M
    DECAY_TILE = DECAY ** TAU
    assert KC == NT == 4 and PRE <= 4 and FB == 16 and NCH % 2 == 0 and M == P

    ctx = ExitStack()
    with ctx:
        def sb(name, shape, dt):
            return ctx.enter_context(nc.sbuf_tensor(name, shape, dt))

        def sem(name):
            return ctx.enter_context(nc.semaphore(name))

        q1_sb = sb("q1_sb", [P, KC, 4, 2, T], F16)
        w2_sb = sb("w2_sb", [P, FB, 2, H], F16)
        q2_in_sb = w2_sb[:].rearrange("p j t h -> p j (t h)").bitcast(I32)
        wqkv_hi = sb("wqkv_hi", [P, KC, QKV], F16)
        wqkv_lo = sb("wqkv_lo", [P, KC, QKV], F16)
        wo_sb = sb("wo_sb", [P, H], F32)
        par = sb("par", [P, 3 * KC + FB + 2 * FB * KC], F32)
        gamma_c = par[:, 0:KC]
        beta_c = par[:, KC:2 * KC]
        b1_c = par[:, 2 * KC:2 * KC + FB]
        s1_c = par[:, 2 * KC + FB:2 * KC + FB + FB * KC]
        s2_c = par[:, 2 * KC + FB + FB * KC:2 * KC + FB + 2 * FB * KC]
        b2_c = par[:, 2 * KC + FB + 2 * FB * KC:]
        gate_c = sb("gate_c", [P, 2], F32)
        b2_half = sb("b2_half", [P, KC], F32)
        quarter_tops = sb("quarter_tops", [P, 4], F32)
        tops = sb("tops", [P, 6], F32)
        all_tops = sb("all_tops", [P, 6], F32)
        top_q1_part = sb("top_q1_part", [P, 1], F32)
        top_q1 = sb("top_q1", [P, 1], F32)
        top_q2_part = sb("top_q2_part", [P, 1], F32)
        top_q2 = sb("top_q2", [P, 1], F32)
        first_top_q2 = sb("first_top_q2", [P, 1], F32)
        slow_q1 = sb("slow_q1", [P, 1], I32)
        q2_quarter_tops = sb("q2_quarter_tops", [P, 4], F32)
        bound = sb("bound", [P, 6], F32)
        pow2 = sb("pow2", [P, 6], F32)
        up = sb("up", [P, 6], F32)
        up_h, up_wqkv, up_q1, up_y, up_w2, up_q2 = (up[:, n:n + 1] for n in range(6))
        mix = sb("mix", [P, 4], F32)
        gamma_s = sb("gamma_s", [P, KC], F32)
        beta_s = sb("beta_s", [P, KC], F32)
        s1_s = sb("s1_s", [P, KC * FB], F32)
        s2_s = sb("s2_s", [P, FB * KC], F32)
        q1_shift = sb("q1_shift", [P, 1], F32)
        q2_shift = sb("q2_shift", [P, 1], F32)
        w2_up = sb("w2_up", [P, 1], F32)
        minus_zero_point = sb("minus_zero_point", [P, 1], F32)
        z_down = sb("z_down", [P, 1], F32)
        top_q = sb("top_q", [P, 1], F32)
        slow_q = sb("slow_q", [P, 1], I32)
        tau_i = sb("tau_i", [P, 2], I32)
        tau_c = sb("tau_c", [P, 2], F32)
        tau_row = sb("tau_row", [P, P], I32)
        decay_c = sb("decay_c", [P, 2], F32)
        powers = sb("powers", [P, 3], F32)
        in_c = sb("in_c", [P, 3], F32)
        ident = sb("ident", [P, P], F32)
        mask = sb("mask", [P, P], F32)
        EPS_AT, MINUS_HALF, HALF, G_SCALE_AT, MINUS_ONE, ONES = range(6)
        row_const = sb("row_const", [P, 7, NT], F32)
        xt = sb("xt", [P, NT, H], F32)
        x_again = sb("x_again", [P, NT, H], F32)
        g_rows = sb("g_rows", [P, NT, H], F32)
        s_rows = sb("s_rows", [P, 2, NT, H], F32)
        g_hi = sb("g_hi", [P, KC, T], F16)
        g_lo = sb("g_lo", [P, KC, T], F16)
        h_full = sb("h_full", [P, 2, T], F32)
        h_hi = sb("h_hi", [P, 2, KC, T], F16)
        h_lo = sb("h_lo", [P, 2, KC, T], F16)
        acc = sb("acc", [P, 2, T], F32)
        y_full = sb("y_full", [P, 2, T], F32)
        y_hi = sb("y_hi", [P, Y_RING, T], F16)
        y_lo = sb("y_lo", [P, Y_RING, T], F16)
        zt = sb("zt", [P, 2, KC, T], F32)
        zt_part = sb("zt_part", [P, 4, T], F32)
        qkv = sb("qkv", [P, 2, QKV], F32)
        qk_t = sb("qk_t", [P, 2 * P], F32)
        s_mask = sb("s_mask", [P, P], F32)
        r_t = sb("r_t", [P, P], F32)
        mem_t = sb("mem_t", [P, M], F32)
        fin = sb("fin", [P, 2, H], F32)
        out_sb = sb("out_sb", [P, 2, H], F32)
        wide = fin
        s2_row = out_sb
        q1_in_sb = [v.rearrange("p (k n) -> p k n", k=KC) for v in
                    (y_hi[:].rearrange("p j n -> p (j n)").bitcast(I32),
                     y_lo[:].rearrange("p j n -> p (j n)").bitcast(I32),
                     zt[:, 0].rearrange("p j n -> p (j n)").bitcast(I32),
                     zt[:, 1].rearrange("p j n -> p (j n)").bitcast(I32))]
        wqkv_in = s_rows[:, 1].rearrange("p i h -> p (i h)")[:, 0:KC * QKV].rearrange("p (k n) -> p k n", k=KC)
        stat6 = sb("stat6", [P, NT, 6], F32)
        mv = sb("mv", [P, 2, NT, 2], F32)
        row_z = sb("row_z", [P, 2, 2, NT], F32)
        rs = row_z[:, :, 0, :]
        nmr = row_z[:, :, 1, :]
        finish_z = sb("finish_z", [P, 2, NT], F32)
        gs = sb("gs", [P, 2, NT], F32)
        v2 = sb("v2", [P, 4, NT], F32)
        row_c = sb("row_c", [P, 2, 3, NT], F32)

        blk = [ctx.enter_context(nc.psum_tensor(f"blk{n}", [P, T], F32)) for n in range(BANKS)]
        side = [ctx.enter_context(nc.psum_tensor(f"side{n}", [P, T], F32)) for n in range(2)]
        blk2 = [ctx.enter_context(nc.psum_tensor(f"blk2_{n}", [P, T], F32)) for n in range(BANKS)]

        first_turn_bank = blk2 + side[:1]

        par_in, wq_in, wo_in, m_in, gate_in = (
            sem(n) for n in ("par_in", "wq_in", "wo_in", "m_in", "gate_in"))
        q1_in = [sem(f"q1_in{n}") for n in range(4)]
        q2_in = [sem(f"q2_in{n}") for n in range(4)]
        s2_in = [sem(f"s2_in{n}") for n in range(2)]
        x_in = sem("x_in")
        x_again_in = [sem(f"x_again_in{n}") for n in range(4)]
        dve_link, pool_link = sem("dve_link"), sem("pool_link")
        gate_done, wo_gated = sem("gate_done"), sem("wo_gated")
        tops_done, all_tops_done = sem("tops_done"), sem("all_tops_done")
        top_q1_done, all_top_q1_done = sem("top_q1_done"), sem("all_top_q1_done")
        q2_quarter, top_q2_done, top_q2_known = sem("q2_quarter"), sem("top_q2_done"), sem("top_q2_known")
        first_top_q2_done, q2_scaled = sem("first_top_q2_done"), sem("q2_scaled")
        h_scales, s1_scaled, q1_scale, wqkv_split = (
            sem(n) for n in ("h_scales", "s1_scaled", "q1_scale", "wqkv_split"))
        ident_done, tau_made, tau_done, decay_done, in_c_done = (
            sem(n) for n in ("ident_done", "tau_made", "tau_done", "decay_done", "in_c_done"))
        slow_known = sem("slow_known")
        q1_wide, q1_hi_done, wqkv_hi_done = sem("q1_wide"), sem("q1_hi_done"), sem("wqkv_hi_done")
        q1_low_zero = sem("q1_low_zero")
        q1_done = [sem(f"q1_done{n}") for n in range(2)]
        row_c_done = sem("row_c_done")
        w2_wide, w2_by_s2, w2_scaled = sem("w2_wide"), sem("w2_by_s2"), sem("w2_scaled")
        w2_scale_done, w2_hi_done, w2_done = sem("w2_scale_done"), sem("w2_hi_done"), sem("w2_done")
        blk_done = sem("blk_done")
        acc_first = sem("acc_first")
        acc_done = sem("acc_done")
        silu_done = sem("silu_done")
        y_hi_done = sem("y_hi_done")
        y_lo_done = sem("y_lo_done")
        blk2_done = sem("blk2_done")
        zt_first = sem("zt_first")
        zt_add = sem("zt_add")
        zt_part_done = sem("zt_part_done")
        zt_part_add = sem("zt_part_add")
        zt_tail, tail_mul, tail_out = sem("zt_tail"), sem("tail_mul"), sem("tail_out")
        z_turned = sem("z_turned")
        finish_z_done = sem("finish_z_done")
        q2_wide, q2_hi_done, q2_done = sem("q2_wide"), sem("q2_hi_done"), sem("q2_done")
        fin_done = sem("fin_done")
        fin_silu = sem("fin_silu")
        fin_mul = sem("fin_mul")
        out_done = sem("out_done")
        out_free = [sem(f"out_free{n}") for n in range(2)]
        bn_done = sem("bn_done")
        mv_done = sem("mv_done")
        rows_step = sem("rows_step")
        rows_done = sem("rows_done")
        g_done = sem("g_done")
        turn_done = sem("turn_done")
        turn_act = sem("turn_act")
        g_lo_done = sem("g_lo_done")
        h_hi_done = sem("h_hi_done")
        h_done = sem("h_done")
        qkv_done = sem("qkv_done")
        qkv_out = sem("qkv_out")
        qkt_done = sem("qkt_done")
        qkt_out = sem("qkt_out")
        scores_done = sem("scores_done")
        masked = sem("masked")
        read_done = sem("read_done")
        r_out = sem("r_out")
        mem_done = sem("mem_done")
        wo_done = sem("wo_done")
        s_out = sem("s_out")

        block = ctx.enter_context(nc.Block())

        def wait(eng, s, count):
            if not (isinstance(count, int) and count <= 0):
                eng.wait_ge(s, count)

        def each_chunk(eng, body):
            body(FIRST, 0, 0)
            with eng.Fori(0, NCH // 2 - 1) as it:
                body(MIDDLE, it * 2 + 1, 1)
                body(MIDDLE, it * 2 + 2, 0)
            body(LAST, NCH - 1, 1)
            body(TAIL, NCH, 0)

        def blk2_count(c, position, g):
            return FC2_BLOCKS * c + fc2_block(position, g) + 1

        def in_tail(c, position):
            return isinstance(c, int) and c == NCH - 1 and position >= TAIL_POSITION

        def by_parts(c, position, hb):
            return position >= PRE and hb >= 1 and not (in_tail(c, position) and hb >= 2)

        def part_count(c, position, hb):
            if in_tail(c, position):
                return part_count(c, TAIL_POSITION - 1, KC - 1) + position - TAIL_POSITION + hb
            return (KC - 1) * ((FB - PRE) * c + position - PRE) + hb

        def part_at(c, parity, position, hb):
            return (parity * (KC - 1) * (FB - PRE) + part_count(c, position, hb) - part_count(c, PRE, 1)) % 4

        def tile_count(c, i):
            return 4 * c + (i // 2 if isinstance(c, int) and c == NCH - 1 else i) + 1

        def tail_count(position, hb):
            return 2 * (position - TAIL_POSITION) + hb - 1

        def fc1_bank(e):
            return blk[bank_of(e, FC1_BLOCKS)]

        def fc2_bank(position, g):
            return blk2[bank_of(fc2_block(position, g), FC2_BLOCKS)]

        @block.sync
        def _(sp):
            def load_x(c):
                for b in range(B):
                    sp.dma_start(xt[b * TAU:(b + 1) * TAU, :, :],
                                 x[b, bass.ds(c * STEPS_T, STEPS_T), :].rearrange("(i t) h -> t i h", t=TAU)
                                 ).then_inc(x_in, 16)

            def load_again(c, i):
                for b in range(B):
                    sp.dma_start(x_again[b * TAU:(b + 1) * TAU, i, :],
                                 x[b, bass.ds(c * STEPS_T + i * TAU, TAU), :]).then_inc(x_again_in[i], 16)

            def store(c, i):
                if i % 2 == 1 and isinstance(c, int) and c == NCH - 1:
                    sp.wait_ge(tail_out, i // 2 + 1)
                else:
                    sp.wait_ge(out_done, tile_count(c, i))
                for b in range(B):
                    sp.dma_start(out[b, bass.ds(c * STEPS_T + i * TAU, TAU), :],
                                 out_sb[b * TAU:(b + 1) * TAU, i % 2, :]).then_inc(out_free[i % 2], 16)

            load_x(0)
            sp.dma_start(wqkv_in, wqkv).then_inc(wq_in, 16)
            for n in range(4):
                sp.dma_start(q1_in_sb[n], q1.rearrange("(g p) (n c) -> n p g c", p=P, n=4)[n]
                             ).then_inc(q1_in[n], 16)
            sp.dma_start(wo_sb[:], wo).then_inc(wo_in, 16)
            sp.dma_start(mem_t[:], m0).then_inc(m_in, 16)
            for n in range(4):
                sp.dma_start(q2_in_sb[:, 4 * n:4 * n + 4, :], q2.rearrange("(n j p) h -> n p j h", n=4, p=P)[n]
                             ).then_inc(q2_in[n], 16)
            for j in range(PRE):
                if j >= 2:
                    sp.wait_ge(w2_by_s2, j - 1)
                sp.dma_start(s2_row[:, j % 2, :], s2[j, :].partition_broadcast(P)).then_inc(s2_in[j % 2], 16)

            def body(kind, c, parity):
                if kind in (FIRST, MIDDLE):
                    sp.wait_ge(g_done, 4 * c + 4)
                    load_x(c + 1)
                if kind != FIRST:
                    for i in range(NT):
                        store(c - 1, i)
                        if kind != TAIL:
                            load_again(c, i)
                else:
                    for i in range(NT):
                        load_again(c, i)

            each_chunk(sp, body)
            for n in range(2):
                sp.wait_ge(out_free[n], 64 * 2 * NCH + 1)

        @block.tensor
        def _(pe):
            def bank_free(kind, c, e):
                (job, i), chunks = job_before(kind, e)
                n = 4 * (c - chunks + {"turn": 1, "turn_z": -1}.get(job, 0)) + i + 1
                read, per_job = {"qkv": (qkv_out, 3), "qkt": (qkt_out, 1), "scores": (masked, 1),
                                 "read": (mem_done, 1), "wo": (s_out, 1), "turn": (g_lo_done, 1),
                                 "turn_z": (fin_done, 1)}[job]
                pe.wait_ge(read, per_job * n)

            def turn(c, k, bank):
                if k == 0:
                    pe.wait_ge(g_done, 4 * c + 4)
                for i in range(NT):
                    mm = pe.transpose(bank[:, i * P:(i + 1) * P], g_rows[:, i, k * P:(k + 1) * P], ident[:])
                mm.then_inc(turn_done, 1)

            def run_side(kind, c, parity, e):
                job, i = SIDE[e]
                bank = side[SIDE_BANK[e]]
                bank_free(kind, c, e)
                if job == "turn_z":
                    if i == 0:
                        pe.wait_ge(zt_add, (FB - PRE) * c)
                        if kind == TAIL:
                            pe.wait_ge(zt_part_add, part_count(NCH - 1, FB - 1, 1))
                            pe.wait_ge(zt_tail, tail_count(FB - 1, KC - 1))
                        else:
                            pe.wait_ge(zt_part_add, (KC - 1) * (FB - PRE) * c)
                    for hb in range(KC):
                        mm = pe.transpose(bank[:, hb * P:(hb + 1) * P], zt[:, 1 - parity, hb, i * P:(i + 1) * P],
                                          ident[:])
                    mm.then_inc(z_turned, 1)
                elif job == "turn":
                    turn(c + 1, i, bank)
                elif job == "qkv":
                    if i == 0:
                        pe.wait_ge(g_lo_done, 4 * c + 4)
                    if kind == FIRST and i == 0:
                        pe.wait_ge(wqkv_split, 1)
                    rows = slice(i * P, (i + 1) * P)
                    for k in range(KC):
                        for n, (a, w) in enumerate(((g_hi, wqkv_hi), (g_lo, wqkv_hi), (g_hi, wqkv_lo))):
                            mm = pe.matmul(bank[:, 0:QKV], a[:, k, rows], w[:, k, :],
                                           start=(k == 0 and n == 0), stop=(k == KC - 1 and n == 2))
                    mm.then_inc(qkv_done, 1)
                elif job == "qkt":
                    pe.wait_ge(qkv_out, 3 * (4 * c + i + 1))
                    pe.transpose(bank[:, 0:P], qkv[:, i % 2, 0:M], ident[:])
                    pe.transpose(bank[:, P:2 * P], qkv[:, i % 2, M:2 * M], ident[:]).then_inc(qkt_done, 1)
                elif job == "scores":
                    pe.wait_ge(qkt_out, 4 * c + i + 1)
                    pe.matmul(bank[:, 0:P], qk_t[:, P:2 * P], qk_t[:, 0:P], start=True, stop=True
                              ).then_inc(scores_done, 1)
                elif job == "read":
                    pe.wait_ge(masked, 4 * c + i + 1)
                    if kind == FIRST and i == 0:
                        pe.wait_ge(m_in, 16)
                    wait(pe, mem_done, 4 * c + i)
                    pe.matmul(bank[:, 0:P], mem_t[:], qk_t[:, 0:P], start=True, stop=False)
                    pe.matmul(bank[:, 0:P], qkv[:, i % 2, 2 * M:3 * M], s_mask[:], start=False, stop=True)
                    pe.matmul(bank[:, P:2 * P], qkv[:, i % 2, M:2 * M], qkv[:, i % 2, 2 * M:3 * M],
                              start=True, stop=True).then_inc(read_done, 1)
                elif job == "wo":
                    pe.wait_ge(r_out, 4 * c + i + 1)
                    if kind == FIRST and i == 0:
                        pe.wait_ge(wo_gated, 1)
                    pe.matmul(bank[:], r_t[:], wo_sb[:], start=True, stop=True).then_inc(wo_done, 1)

            def ffn1(c, parity, j, g, slow, first):
                e = 4 * j + g
                before, chunks = block_before(e, FC1_BLOCKS)
                if before % 4 == 0:
                    wait(pe, acc_first, 16 * (c - chunks) + before // 4 + 1)
                else:
                    wait(pe, acc_done, 48 * (c - chunks) + 3 * (before // 4) + before % 4)
                if j == 0:
                    pe.wait_ge(h_done, 4 * c + g + 1)
                if first:
                    pe.wait_ge(q1_done[g % 2], 2 * (j // 4) + g // 2 + 1)
                terms = [(0, h_hi), (0, h_lo)] + ([(1, h_hi)] if slow else [])
                for n, (w, a) in enumerate(terms):
                    mm = pe.matmul(fc1_bank(e)[:], q1_sb[:, g, j // 4, w, j % 4 * P:(j % 4 + 1) * P],
                                   a[:, parity, g, :],
                                   start=(n == 0), stop=(n == len(terms) - 1))
                mm.then_inc(blk_done, 1)

            def ffn2(c, position, g, slow, first):
                hb, j = before_of(position, g) if position < PRE else (g, position)
                if position >= PRE or j == 0:
                    before, chunks = block_before(fc2_block(position, g), FC2_BLOCKS)
                    n, hidden = divmod(before - KC, KC)
                    if before < KC:
                        wait(pe, zt_first, KC * (c - chunks) + before + 1)
                    elif hidden == 0:
                        wait(pe, zt_add, (FB - PRE) * (c - chunks) + n + 1)
                    elif by_parts(c - chunks, n + PRE, hidden):
                        wait(pe, zt_part_done, part_count(c - chunks, n + PRE, hidden))
                    else:
                        pe.wait_ge(zt_tail, tail_count(n + PRE, hidden))
                if hb == 0:
                    pe.wait_ge(y_lo_done, FB * c + j + 1)
                if position < PRE:
                    terms = [(0, y_hi), (0, y_lo), (1, y_hi)]
                    if first and hb == 0:
                        pe.wait_ge(w2_done, j + 1)
                else:
                    terms = [(0, y_hi), (0, y_lo)] + ([(1, y_hi)] if slow else [])
                    if first and hb == 0:
                        pe.wait_ge(q2_done, j - PRE + 1)
                for n, (part, y) in enumerate(terms):
                    mm = pe.matmul(fc2_bank(position, g)[:], w2_sb[:, j, part, hb * P:(hb + 1) * P],
                                   y[:, j % Y_RING, :],
                                   start=(n == 0 and (position >= PRE or j == 0)),
                                   stop=(n == len(terms) - 1 and (position >= PRE or j == PRE - 1)))
                if position >= PRE or j == PRE - 1:
                    mm.then_inc(blk2_done, 1)

            def step(kind, c, parity, e, slow):
                if kind != TAIL:
                    ffn1(c, parity, e // 4, e % 4, slow, kind == FIRST)
                if todo := fc2_at(kind, e):
                    chunk, position, g = todo
                    ffn2(c + chunk, position, g, slow, kind == FIRST or chunk < 0)
                if has_job(kind, e):
                    run_side(kind, c, parity, e)

            def first_steps(slow):
                for e in range(FIRST_STEPS):
                    step(FIRST, 0, 0, e, slow)

            def other_steps(slow):
                def body(kind, c, parity):
                    for e in range(FIRST_STEPS if kind == FIRST else 0, STEPS):
                        step(kind, c, parity, e, slow)
                each_chunk(pe, body)

            pe.wait_ge(ident_done, 2)
            for k in range(KC):
                turn(0, k, first_turn_bank[k])
            pe.wait_ge(q1_low_zero, 1)
            pe.wait_ge(q1_scale, 1)
            slow = pe.value_load(slow_q1[0:1, 0:1], min_val=0, max_val=1)
            with pe.If(slow > 0):
                first_steps(True)
            with pe.Else():
                first_steps(False)
            pe.wait_ge(slow_known, 1)
            slow = pe.value_load(slow_q[0:1, 0:1], min_val=0, max_val=1)
            with pe.If(slow > 0):
                other_steps(True)
            with pe.Else():
                other_steps(False)

        @block.scalar
        def _(act):
            act.dma_start(par[:], params).then_inc(par_in, 16)
            act.dma_start(gate_c[:, 0:1], gate.partition_broadcast(P)).then_inc(gate_in, 16)
            act.wait_ge(gate_in, 16)
            act.activation(gate_c[:, 1:2], gate_c[:, 0:1], ACT.Sigmoid).then_inc(gate_done, 1)

            def turned(c, k, bank):
                act.wait_ge(turn_done, 4 * c + k + 1)
                wait(act, qkv_done, 4 * c)
                act.activation(g_hi[:, k, :], bank[:], ACT.Copy).then_inc(turn_act, 1)
                if isinstance(c, int) and c == 0 and k == 0:
                    act.wait_ge(h_scales, 1)
                wait(act, h_done, 4 * c + k - 1)
                act.activation(h_full[:, k % 2, :], bank[:], ACT.Identity,
                               bias=beta_s[:, k:k + 1], scale=gamma_s[:, k:k + 1]).then_inc(turn_act, 1)

            def side_out(c, parity, e):
                job, i = SIDE[e]
                bank = side[SIDE_BANK[e]]
                if job == "turn":
                    turned(c + 1, i, bank)
                elif job == "qkv":
                    act.wait_ge(qkv_done, 4 * c + i + 1)
                    act.wait_ge(row_c_done, c + 1)
                    wait(act, read_done, 4 * c + i - 1)
                    for n in range(3):
                        act.activation(qkv[:, i % 2, n * M:(n + 1) * M], bank[:, n * M:(n + 1) * M], ACT.Copy,
                                       scale=row_c[:, parity, n, i:i + 1]).then_inc(qkv_out, 1)
                elif job == "qkt":
                    act.wait_ge(qkt_done, 4 * c + i + 1)
                    wait(act, read_done, 4 * c + i)
                    act.activation(qk_t[:], bank[:, 0:2 * P], ACT.Copy).then_inc(qkt_out, 1)
                elif job == "read":
                    act.wait_ge(read_done, 4 * c + i + 1)
                    wait(act, wo_done, 4 * c + i)
                    act.activation(r_t[:], bank[:, 0:P], ACT.Copy).then_inc(r_out, 1)
                elif job == "wo":
                    act.wait_ge(wo_done, 4 * c + i + 1)
                    act.activation(s_rows[:, parity, i, :], bank[:], ACT.Copy).then_inc(s_out, 1)

            def first_block(c, j):
                act.wait_ge(blk_done, 64 * c + 4 * j + 1)
                wait(act, silu_done, 16 * c + j - 1)
                act.activation(acc[:, j % 2, :], fc1_bank(4 * j)[:], ACT.Identity, bias=b1_c[:, j:j + 1],
                               scale=s1_s[:, j:j + 1]).then_inc(acc_first, 1)

            def silu(c, j, high):
                act.wait_ge(acc_done, 48 * c + 3 * j + 3)
                wait(act, y_lo_done, 16 * c + j - 1)
                act.activation(y_full[:, j % 2, :], acc[:, j % 2, :], ACT.Silu).then_inc(silu_done, 1)
                if not high:
                    return
                act.wait_ge(silu_done, 16 * c + j + 1)
                if j >= Y_RING:
                    act.wait_ge(blk2_done, blk2_count(c, max(j - Y_RING, PRE - 1), KC - 1))
                act.activation(y_hi[:, j % Y_RING, :], y_full[:, j % 2, :], ACT.Copy, scale=up_y
                               ).then_inc(y_hi_done, 1)

            def block_out(c, parity, position, g):
                if position < PRE:
                    hb, j = before_of(position, g)
                    if j == PRE - 1:
                        act.wait_ge(blk2_done, blk2_count(c, position, g))
                        act.activation(zt[:, parity, hb, :], fc2_bank(position, g)[:], ACT.Identity,
                                       bias=b2_half[:, hb:hb + 1], scale=z_down[:, 0:1]
                                       ).then_inc(zt_first, 1)
                elif by_parts(c, position, g):
                    act.wait_ge(blk2_done, blk2_count(c, position, g))
                    wait(act, zt_part_add, part_count(c, position, g) - 4)
                    act.activation(zt_part[:, part_at(c, parity, position, g), :], fc2_bank(position, g)[:], ACT.Copy,
                                   scale=s2_s[:, KC * position + g:KC * position + g + 1]).then_inc(zt_part_done, 1)

            def gate_silu(c, parity, i):
                act.wait_ge(fin_done, 4 * c + i + 1)
                act.activation(fin[:, i % 2, :], fin[:, i % 2, :], ACT.Silu, bias=finish_z[:, 1, i:i + 1]
                               ).then_inc(fin_silu, 1)

            def body(kind, c, parity):
                for e in range(STEPS):
                    j, g = e // 4, e % 4
                    if has_job(kind, e - 1) and SIDE[e - 1][0] not in ("scores", "turn_z", "turn"):
                        side_out(c, parity, e - 1)
                    if todo := fc2_at(kind, e - 1):
                        chunk, position, g2 = todo
                        block_out(c + chunk, (parity + chunk) % 2, position, g2)
                    if kind != TAIL and g == 0:
                        first_block(c, j)
                    if has_job(kind, e - 1) and SIDE[e - 1][0] == "turn":
                        side_out(c, parity, e - 1)
                    if g == SILU_G and (kind != TAIL and j >= 1 or e == SILU_G and kind != FIRST):
                        silu(*(c, j - 1) if j >= 1 else (c - 1, FB - 1), kind == FIRST)
                    if has_job(kind, e - FIN_LAG) and SIDE[e - FIN_LAG][0] == "turn_z":
                        gate_silu(c - 1, 1 - parity, SIDE[e - FIN_LAG][1])
                    if kind == FIRST and e in W2_AT:
                        n = W2_AT.index(e)
                        act.wait_ge(q2_in[n // 4], 16)
                        if n >= 2:
                            act.wait_ge(w2_done, n - 1)
                        act.activation(wide[:, n % 2, :], q2_in_sb[:, n, :], ACT.Identity,
                                       bias=minus_zero_point[:, 0:1]).then_inc(w2_wide, 1)
                    if kind == FIRST and e - 3 in W2_AT:
                        n = W2_AT.index(e - 3)
                        if n == 0:
                            act.wait_ge(w2_scale_done, 1)
                        act.wait_ge(w2_by_s2, n + 1)
                        act.activation(wide[:, n % 2, :], wide[:, n % 2, :], ACT.Copy, scale=w2_up[:, 0:1]
                                       ).then_inc(w2_scaled, 1)
                        act.wait_ge(w2_scaled, n + 1)
                        act.activation(w2_sb[:, n, 0, :], wide[:, n % 2, :], ACT.Copy).then_inc(w2_hi_done, 1)
                    if kind == FIRST and e in Q2_AT:
                        n = Q2_AT.index(e)
                        if n == 0:
                            act.wait_ge(q2_scaled, 1)
                            act.wait_ge(w2_done, PRE)
                        if n >= 2:
                            act.wait_ge(q2_done, n - 1)
                        act.activation(wide[:, n % 2, :], q2_in_sb[:, PRE + n, :], ACT.Identity,
                                       bias=q2_shift[:, 0:1], scale=up_q2).then_inc(q2_wide, 1)

            for k in range(KC):
                turned(0, k, first_turn_bank[k])
            act.activation(wqkv_hi[:], wqkv_in, ACT.Copy, scale=up_wqkv).then_inc(wqkv_hi_done, 1)

            def q1_pieces(slow):
                for n in range(FB):
                    g, quarter = n % 4, n // 4
                    if slow:
                        if n >= 2:
                            act.wait_ge(q1_done[n % 2], n // 2)
                        act.activation(wide[:, n % 2, :], q1_in_sb[quarter][:, g, :], ACT.Identity,
                                       bias=q1_shift[:, 0:1], scale=up_q1).then_inc(q1_wide, 1)
                    elif g % 2 == 0:
                        act.activation(q1_sb[:, g, quarter, 0, :], q1_in_sb[quarter][:, g, :], ACT.Identity,
                                       bias=q1_shift[:, 0:1], scale=up_q1).then_inc(q1_done[0], 1)

            act.wait_ge(q1_scale, 1)
            slow = act.value_load(slow_q1[0:1, 0:1], min_val=0, max_val=1)
            with act.If(slow > 0):
                q1_pieces(True)
            with act.Else():
                q1_pieces(False)
            act.wait_ge(wo_in, 16)
            act.wait_ge(gate_done, 1)
            act.activation(wo_sb[:], wo_sb[:], ACT.Copy, scale=gate_c[:, 1:2]).then_inc(wo_gated, 1)
            act.wait_ge(s1_scaled, 1)
            each_chunk(act, body)

        @block.vector
        def _(dve):
            def stats(c, i):
                if i == 0:
                    dve.wait_ge(x_in, 64 * (c + 1))
                dve.bn_stats(stat6[:, i, :], xt[:, i, :]).then_inc(bn_done, 1)

            def moments(c, parity, i):
                dve.bn_aggr(mv[:, parity, i, :], stat6[:, i, :]).then_inc(mv_done, 1)

            def normalise(c, parity, i):
                if i == 0:
                    dve.wait_ge(rows_done, c + 1)
                    wait(dve, turn_done, 4 * c)
                dve.tensor_scalar(g_rows[:, i, :], xt[:, i, :], mv[:, parity, i, 0:1],
                                  gs[:, parity, i:i + 1], ALU.subtract, ALU.mult).then_inc(g_done, 1)

            def turned_low(c, parity, k, bank):
                dve.wait_ge(turn_act, 2 * (4 * c + k + 1))
                dve.tensor_tensor(g_lo[:, k, :], bank[:], g_hi[:, k, :], ALU.subtract
                                  ).then_inc(g_lo_done, 1)
                if k == 0:
                    wait(dve, blk_done, 64 * (c - 1))
                dve.tensor_copy(h_hi[:, parity, k, :], h_full[:, k % 2, :]).then_inc(h_hi_done, 1)

            def side_out(c, parity, e):
                job, i = SIDE[e]
                bank = side[SIDE_BANK[e]]
                if job == "turn":
                    turned_low(c + 1, 1 - parity, i, bank)
                elif job == "turn_z":
                    finish(c - 1, 1 - parity, i)
                elif job == "scores":
                    dve.wait_ge(scores_done, 4 * c + i + 1)
                    wait(dve, read_done, 4 * c + i)
                    dve.tensor_tensor(s_mask[:], bank[:, 0:P], mask[:], ALU.mult).then_inc(masked, 1)
                elif job == "read":
                    dve.wait_ge(r_out, 4 * c + i + 1)
                    wait(dve, mem_done, 4 * c + i)
                    dve.scalar_tensor_tensor(mem_t[:], mem_t[:], DECAY_TILE, bank[:, P:2 * P], ALU.mult, ALU.add
                                             ).then_inc(mem_done, 1)

            def add_block(c, j, g):
                dve.wait_ge(blk_done, 64 * c + 4 * j + g + 1)
                if g == 1:
                    dve.wait_ge(acc_first, 16 * c + j + 1)
                else:
                    dve.wait_ge(acc_done, 48 * c + 3 * j + g - 1)
                dve.scalar_tensor_tensor(acc[:, j % 2, :], fc1_bank(4 * j + g)[:], s1_s[:, g * FB + j:g * FB + j + 1],
                                         acc[:, j % 2, :], ALU.mult, ALU.add).then_inc(acc_done, 1)

            def y_high(c, j):
                dve.wait_ge(silu_done, 16 * c + j + 1)
                if j >= Y_RING:
                    dve.wait_ge(blk2_done, blk2_count(c, max(j - Y_RING, PRE - 1), KC - 1))
                else:
                    wait(dve, blk2_done, 0 if isinstance(c, int) and c == 0
                         else blk2_count(c - 1, j + FB - Y_RING, KC - 1))
                dve.tensor_scalar(y_hi[:, j % Y_RING, :], y_full[:, j % 2, :], up_y, None, ALU.mult
                                  ).then_inc(y_hi_done, 1)

            def y_low(c, j):
                dve.wait_ge(y_hi_done, 16 * c + j + 1)
                dve.scalar_tensor_tensor(y_lo[:, j % Y_RING, :], y_full[:, j % 2, :], up_y,
                                         y_hi[:, j % Y_RING, :],
                                         ALU.mult, ALU.subtract).then_inc(y_lo_done, 1)

            def add_block2(c, parity, j, hb):
                dve.wait_ge(blk2_done, blk2_count(c, j, hb))
                if hb >= 1 and j == TAIL_POSITION:
                    dve.wait_ge(zt_part_add, part_count(c, j - 1, hb))
                elif hb >= 1:
                    dve.wait_ge(zt_tail, tail_count(j - 1, hb))
                elif j == PRE:
                    dve.wait_ge(zt_first, KC * c + 1)
                else:
                    dve.wait_ge(zt_add, (FB - PRE) * c + j - PRE)
                dve.scalar_tensor_tensor(zt[:, parity, hb, :], fc2_bank(j, hb)[:],
                                         s2_s[:, KC * j + hb:KC * j + hb + 1], zt[:, parity, hb, :],
                                         ALU.mult, ALU.add).then_inc(zt_add if hb == 0 else zt_tail, 1)

            def tail_output(c, parity, i):
                dve.wait_ge(fin_silu, 4 * c + i + 1)
                dve.wait_ge(s_out, 4 * c + i + 1)
                dve.wait_ge(out_free[1], 64 * (2 * c + i // 2) + 1)
                dve.tensor_tensor(out_sb[:, 1, :], fin[:, 1, :], s_rows[:, parity, i, :], ALU.mult
                                  ).then_inc(tail_mul, 1)
                dve.wait_ge(tail_mul, i // 2 + 1)
                dve.tensor_tensor(out_sb[:, 1, :], out_sb[:, 1, :], x_again[:, i, :], ALU.add
                                  ).then_inc(tail_out, 1)

            def finish(c, parity, i):
                if i == 0:
                    dve.wait_ge(finish_z_done, c + 1)
                dve.wait_ge(z_turned, 4 * c + i + 1)
                dve.wait_ge(x_again_in[i], 64 * (c + 1))
                if i == 3 and isinstance(c, int) and c == NCH - 1:
                    dve.wait_ge(tail_mul, 1)
                elif i >= 2:
                    dve.wait_ge(fin_mul, 4 * c + i - 1)
                else:
                    dve.wait_ge(x_again_in[i + 2], 64 * (c + 1))
                dve.scalar_tensor_tensor(fin[:, i % 2, :], x_again[:, i, :], finish_z[:, 0, i:i + 1],
                                         side[SIDE_BANK[STEP_OF["turn_z", i]]][:], ALU.mult, ALU.add
                                         ).then_inc(fin_done, 1)

            def top_of_q2(n):
                dve.wait_ge(q2_in[n], 16)
                dve.tensor_reduce(q2_quarter_tops[:, n:n + 1], q2_in_sb[:, 4 * n:4 * n + 4, :], AX.XY, ALU.max,
                                  apply_absolute_value=True).then_inc(q2_quarter, 1)
                if n == 3:
                    dve.wait_ge(q2_quarter, 4)
                    dve.tensor_reduce(top_q2_part[:], q2_quarter_tops[:], AX.X, ALU.max).then_inc(top_q2_done, 1)

            def w2_scale():
                dve.wait_ge(first_top_q2_done, 1)
                link(dve.tensor_scalar(mix[:, 0:1], first_top_q2[:], ZERO_POINT, None, ALU.add))
                link(dve.tensor_scalar(mix[:, 1:2], mix[:, 0:1], top_s2, 0.5, ALU.mult, ALU.mult))
                link(dve.tensor_scalar(bound[:, 4:5], mix[:, 1:2], TINY, None, ALU.max))
                power_of_two(slice(4, 5))
                dve.tensor_scalar(z_down[:], pow2[:, 4:5], pow2[:, 3:4], 1.0 / (TOP * TOP), ALU.mult, ALU.mult)
                dve.tensor_scalar(w2_up[:], up_w2, 0.5, None, ALU.mult).then_inc(w2_scale_done, 1)

            def q2_scale():
                dve.wait_ge(top_q2_known, 1)
                link(dve.tensor_scalar(top_q[:], top_q1[:], top_q2[:], None, ALU.max))
                dve.tensor_scalar(slow_q[:], top_q[:], EXACT_Q, None, ALU.is_gt).then_inc(slow_known, 1)
                link(dve.tensor_scalar(bound[:, 5:6], top_q2[:], ZERO_POINT, None, ALU.add))
                power_of_two(slice(5, 6))
                link(dve.tensor_scalar(mix[:, 0:1], pow2[:, 5:6], pow2[:, 3:4], 0.5 / (TOP * TOP),
                                       ALU.mult, ALU.mult))
                dve.tensor_scalar(s2_s[:], s2_c, mix[:, 0:1], None, ALU.mult)
                dve.tensor_scalar(q2_shift[:], up_q2, -ZERO_POINT, None, ALU.mult).then_inc(q2_scaled, 1)

            def q2_high(n):
                dve.wait_ge(q2_wide, n + 1)
                dve.tensor_copy(w2_sb[:, PRE + n, 0, :], wide[:, n % 2, :]).then_inc(q2_hi_done, 1)

            def body(kind, c, parity):
                for e in range(STEPS):
                    j, g = e // 4, e % 4
                    ahead = kind in (FIRST, MIDDLE)
                    if ahead and e == MOMENTS_AT[0]:
                        dve.wait_ge(bn_done, 4 * (c + 1) + NT)
                    if kind != TAIL and g >= 1:
                        add_block(c, j, g)
                    todo = fc2_at(kind, e)
                    if todo and todo[1] >= PRE and not by_parts(c + todo[0], todo[1], g):
                        add_block2(c + todo[0], (parity + todo[0]) % 2, todo[1], g)
                    if has_job(kind, e - 1) and SIDE[e - 1][0] in ("turn_z", "scores"):
                        side_out(c, parity, e - 1)
                    if kind == TAIL and has_job(kind, e - OUT_LAG) and SIDE[e - OUT_LAG][0] == "turn_z":
                        if SIDE[e - OUT_LAG][1] % 2 == 1:
                            tail_output(c - 1, 1 - parity, SIDE[e - OUT_LAG][1])
                    for job, lag in (("turn", TURN_LAG), ("read", READ_LAG)):
                        if has_job(kind, e - lag) and SIDE[e - lag][0] == job:
                            side_out(c, parity, e - lag)
                    if kind != FIRST and g == SILU_G and (kind != TAIL and j >= 1 or e == SILU_G and kind != FIRST):
                        y_high(*(c, j - 1) if j >= 1 else (c - 1, FB - 1))
                    if g == YLOW_G and (kind != TAIL and j >= 1 or e == YLOW_G and kind != FIRST):
                        y_low(*(c, j - 1) if j >= 1 else (c - 1, FB - 1))
                    if kind == FIRST:
                        if e == W2_SCALE_AT:
                            w2_scale()
                        if e in TOP_Q2_AT:
                            top_of_q2(TOP_Q2_AT.index(e) + 1)
                        if e == Q2_SCALE_AT:
                            q2_scale()
                        if e - 1 in Q2_AT:
                            q2_high(Q2_AT.index(e - 1))
                    if ahead and e in STATS_AT:
                        stats(c + 1, STATS_AT.index(e))
                    if ahead and e in MOMENTS_AT:
                        for i in (0, 1):
                            moments(c + 1, 1 - parity, 2 * MOMENTS_AT.index(e) + i)
                    if ahead and e in NORMALISE_AT:
                        normalise(c + 1, 1 - parity, NORMALISE_AT.index(e))

            links = [0]

            def link(ins):
                links[0] += 1
                ins.then_inc(dve_link, 1)
                dve.wait_ge(dve_link, links[0])

            def power_of_two(n):
                link(dve.tensor_scalar(pow2[:, n].bitcast(I32), bound[:, n].bitcast(I32), 0x7F800000, None,
                                       ALU.bitwise_and))
                link(dve.reciprocal(up[:, n], pow2[:, n]))
                link(dve.tensor_scalar(up[:, n], up[:, n], TOP, None, ALU.mult))

            def top(n, src, axis=AX.X):
                return dve.tensor_reduce(tops[:, n:n + 1], src, axis, ALU.max, apply_absolute_value=True)

            dve.wait_ge(tau_made, 2)
            link(dve.tensor_scalar(tau_i[:, 1:2], tau_i[:, 0:1], TAU - 1, None, ALU.bitwise_and))
            link(dve.tensor_copy(tau_c[:, 0:1], tau_i[:, 1:2]))
            link(dve.tensor_scalar(tau_c[:, 1:2], tau_c[:, 0:1], -1.0, float(TAU - 1), ALU.mult, ALU.add))
            dve.tensor_scalar(mask[:], tau_row[:], tau_c[:, 0:1], 1.0 / DECAY_TILE, ALU.is_gt, ALU.mult
                              ).then_inc(tau_done, 1)
            def top_of_q1(n):
                dve.wait_ge(q1_in[n], 16)
                return dve.tensor_reduce(quarter_tops[:, n:n + 1], q1_in_sb[n], AX.XY, ALU.max,
                                         apply_absolute_value=True)

            for i in range(NT):
                stats(0, i)
            dve.wait_ge(bn_done, NT)
            for i in range(NT):
                moments(0, 0, i)
            dve.wait_ge(par_in, 16)
            top(0, gamma_c)
            top(1, beta_c)
            top(2, s1_c)
            top(3, b1_c)
            top(5, s2_c)
            dve.wait_ge(wq_in, 16)
            top(4, wqkv_in, AX.XY).then_inc(tops_done, 1)
            top_of_q1(0)
            for i in range(NT):
                normalise(0, 0, i)
            dve.wait_ge(all_tops_done, 1)
            top_gamma, top_beta, top_s1, top_b1, top_wqkv, top_s2 = (all_tops[:, n:n + 1] for n in range(6))
            dve.scalar_tensor_tensor(bound[:, 0:1], top_gamma, float(H) ** 0.5, top_beta, ALU.mult, ALU.add)
            link(dve.tensor_copy(bound[:, 1:2], top_wqkv))
            link(dve.tensor_scalar(bound[:, 0:2], bound[:, 0:2], TINY, None, ALU.max))
            power_of_two(slice(0, 2))
            dve.tensor_scalar(gamma_s[:], gamma_c, up_h, 1.0 / G_SCALE, ALU.mult, ALU.mult)
            dve.tensor_scalar(beta_s[:], beta_c, up_h, None, ALU.mult).then_inc(h_scales, 1)
            dve.wait_ge(decay_done, 1)
            link(dve.tensor_scalar(mix[:, 3:4], pow2[:, 1:2], 1.0 / (TOP * G_SCALE), None, ALU.mult))
            dve.tensor_tensor(in_c[:, 0:1], powers[:, 0:1], mix[:, 3:4], ALU.mult)
            dve.tensor_scalar(in_c[:, 1:2], powers[:, 1:2], mix[:, 3:4], 1.0 / B, ALU.mult, ALU.mult)
            dve.tensor_copy(in_c[:, 2:3], mix[:, 3:4]).then_inc(in_c_done, 1)
            for n in range(1, 4):
                turned_low(0, 0, n - 1, first_turn_bank[n - 1])
                last = top_of_q1(n)
            link(last)
            dve.tensor_reduce(top_q1_part[:], quarter_tops[:], AX.X, ALU.max).then_inc(top_q1_done, 1)
            turned_low(0, 0, 3, first_turn_bank[3])
            dve.wait_ge(all_top_q1_done, 1)
            dve.tensor_scalar(slow_q1[:, 0:1], top_q1[:], EXACT_Q, None, ALU.is_gt)
            link(dve.tensor_scalar(bound[:, 2:3], top_q1[:], ZERO_POINT, None, ALU.add))
            power_of_two(slice(2, 3))
            dve.tensor_scalar(q1_shift[:], up_q1, -ZERO_POINT, None, ALU.mult).then_inc(q1_scale, 1)
            link(dve.tensor_tensor(mix[:, 2:3], pow2[:, 0:1], pow2[:, 2:3], ALU.mult))
            dve.tensor_scalar(s1_s[:], s1_c, mix[:, 2:3], 1.0 / (TOP * TOP), ALU.mult, ALU.mult).then_inc(s1_scaled, 1)

            def q1_parts(slow):
                if slow:
                    dve.wait_ge(q1_low_zero, 1)
                for n in range(FB):
                    g, quarter = n % 4, n // 4
                    if slow:
                        dve.wait_ge(q1_wide, n + 1)
                        dve.tensor_copy(q1_sb[:, g, quarter, 0, :], wide[:, n % 2, :]).then_inc(q1_hi_done, 1)
                        dve.wait_ge(q1_hi_done, n + 1)
                        dve.tensor_tensor(q1_sb[:, g, quarter, 1, :], wide[:, n % 2, :],
                                          q1_sb[:, g, quarter, 0, :], ALU.subtract).then_inc(q1_done[n % 2], 1)
                    elif g % 2 == 1:
                        dve.tensor_scalar(q1_sb[:, g, quarter, 0, :], q1_in_sb[quarter][:, g, :], -ZERO_POINT,
                                          up_q1, ALU.add, ALU.mult).then_inc(q1_done[1], 1)
                    if n == 3:
                        dve.wait_ge(wqkv_hi_done, 1)
                        dve.scalar_tensor_tensor(wqkv_lo[:].rearrange("p k n -> p (k n)"),
                                                 wqkv_in.rearrange("p k n -> p (k n)"), up_wqkv,
                                                 wqkv_hi[:].rearrange("p k n -> p (k n)"), ALU.mult, ALU.subtract
                                                 ).then_inc(wqkv_split, 1)

            slow = dve.value_load(slow_q1[0:1, 0:1], min_val=0, max_val=1)
            with dve.If(slow > 0):
                q1_parts(True)
            with dve.Else():
                q1_parts(False)
            link(dve.tensor_scalar(mix[:, 0:1], top_gamma, top_beta, float(H), ALU.add, ALU.mult))
            link(dve.tensor_tensor(mix[:, 1:2], mix[:, 0:1], bound[:, 2:3], ALU.mult))
            link(dve.tensor_scalar(bound[:, 3:4], mix[:, 1:2], top_s1, top_b1, ALU.mult, ALU.add))
            link(dve.tensor_scalar(bound[:, 3:4], bound[:, 3:4], TINY, None, ALU.max))
            power_of_two(slice(3, 4))
            dve.tensor_scalar(b2_half[:], b2_c, 0.5, None, ALU.mult)
            top_of_q2(0)
            each_chunk(dve, body)

        @block.gpsimd
        def _(pool):
            links = [0]

            def link(ins):
                links[0] += 1
                ins.then_inc(pool_link, 1)
                pool.wait_ge(pool_link, links[0])

            def rows(c, parity):
                pool.wait_ge(mv_done, 4 * c + 4)
                mean, var = mv[:, parity, :, 0], mv[:, parity, :, 1]
                t = [v2[:, n, :] for n in range(4)]
                count = [ROW_STEPS * c]

                def step(ins):
                    count[0] = count[0] + 1
                    ins.then_inc(rows_step, 1)
                    pool.wait_ge(rows_step, count[0])

                step(pool.tensor_tensor(t[0], var, row_const[:, EPS_AT, :], ALU.add))
                step(pool.tensor_tensor(rs[:, parity, :], t[0], row_const[:, MINUS_HALF, :], ALU.pow))
                step(pool.tensor_tensor(t[1], var, rs[:, parity, :], ALU.mult))
                step(pool.tensor_tensor(t[2], t[1], rs[:, parity, :], ALU.mult))
                step(pool.tensor_tensor(t[3], t[2], row_const[:, EPS_AT, :], ALU.add))
                step(pool.tensor_tensor(t[0], t[3], row_const[:, MINUS_HALF, :], ALU.pow))
                step(pool.tensor_tensor(t[1], t[3], row_const[:, HALF, :], ALU.pow))
                step(pool.tensor_tensor(t[2], t[0], rs[:, parity, :], ALU.mult))
                step(pool.tensor_tensor(gs[:, parity, :], t[2], row_const[:, G_SCALE_AT, :], ALU.mult))
                step(pool.tensor_tensor(t[3], mean, rs[:, parity, :], ALU.mult))
                pool.tensor_tensor(nmr[:, parity, :], t[3], row_const[:, MINUS_ONE, :], ALU.mult
                                   ).then_inc(rows_done, 1)

            def row_scales(c, parity):
                if isinstance(c, int) and c == 0:
                    pool.wait_ge(in_c_done, 1)
                for n in range(3):
                    last = pool.tensor_tensor(row_c[:, parity, n, :], v2[:, 1, :],
                                              in_c[:, n:n + 1].to_broadcast([P, NT]), ALU.mult)
                last.then_inc(row_c_done, 1)

            def h_low(c, parity, k):
                pool.wait_ge(h_hi_done, 4 * c + k + 1)
                pool.tensor_tensor(h_lo[:, parity, k, :], h_full[:, k % 2, :], h_hi[:, parity, k, :], ALU.subtract
                                   ).then_inc(h_done, 1)

            def w2_by_scale(n):
                pool.wait_ge(w2_wide, n + 1)
                pool.wait_ge(s2_in[n % 2], 16 * (n // 2 + 1))
                pool.tensor_tensor(wide[:, n % 2, :], wide[:, n % 2, :], s2_row[:, n % 2, :], ALU.mult
                                   ).then_inc(w2_by_s2, 1)

            def w2_low(n):
                pool.wait_ge(w2_hi_done, n + 1)
                pool.tensor_tensor(w2_sb[:, n, 1, :], wide[:, n % 2, :], w2_sb[:, n, 0, :], ALU.subtract
                                   ).then_inc(w2_done, 1)

            def q2_low(n):
                pool.wait_ge(q2_hi_done, n + 1)
                pool.tensor_tensor(w2_sb[:, PRE + n, 1, :], wide[:, n % 2, :], w2_sb[:, PRE + n, 0, :], ALU.subtract
                                   ).then_inc(q2_done, 1)

            def output(c, parity, i):
                at = tile_count(c, i)
                pool.wait_ge(fin_silu, 4 * c + i + 1)
                pool.wait_ge(s_out, 4 * c + i + 1)
                pool.wait_ge(out_free[i % 2], 64 * (2 * c + i // 2) + 1)
                pool.tensor_tensor(out_sb[:, i % 2, :], fin[:, i % 2, :], s_rows[:, parity, i, :], ALU.mult
                                   ).then_inc(fin_mul, 1)
                pool.wait_ge(fin_mul, at)
                pool.tensor_tensor(out_sb[:, i % 2, :], out_sb[:, i % 2, :], x_again[:, i, :], ALU.add
                                   ).then_inc(out_done, 1)

            def add_part(c, parity, j, hb):
                pool.wait_ge(zt_part_done, part_count(c, j, hb))
                if j == PRE:
                    pool.wait_ge(zt_first, KC * c + hb + 1)
                else:
                    pool.wait_ge(zt_part_add, part_count(c, j - 1, hb))
                pool.tensor_tensor(zt[:, parity, hb, :], zt[:, parity, hb, :], zt_part[:, part_at(c, parity, j, hb), :],
                                   ALU.add).then_inc(zt_part_add, 1)

            def finish_scales(c, parity):
                pool.wait_ge(rows_done, c + 1)
                pool.tensor_tensor(finish_z[:], row_z[:, parity], row_const[:, ONES:ONES + 2, :], ALU.mult
                                   ).then_inc(finish_z_done, 1)

            def body(kind, c, parity):
                for e in range(STEPS):
                    if e == 0 and kind != FIRST:
                        finish_scales(c - 1, 1 - parity)
                    if kind == FIRST and e - 1 in W2_AT:
                        w2_by_scale(W2_AT.index(e - 1))
                    if kind == FIRST and e - 4 in W2_AT:
                        w2_low(W2_AT.index(e - 4))
                    if kind == FIRST and e - 2 in Q2_AT:
                        q2_low(Q2_AT.index(e - 2))
                    if kind == FIRST and e == Q2_SCALE_AT - 1:
                        pool.wait_ge(top_q2_done, 1)
                        pool.partition_all_reduce(top_q2[:], top_q2_part[:], P, bass.bass_isa.ReduceOp.max
                                                  ).then_inc(top_q2_known, 1)
                    todo = fc2_at(kind, e - PART_LAG)
                    if todo and by_parts(c + todo[0], todo[1], todo[2]):
                        add_part(c + todo[0], (parity + todo[0]) % 2, todo[1], todo[2])
                    if has_job(kind, e - OUT_LAG) and SIDE[e - OUT_LAG][0] == "turn_z" and not (
                            kind == TAIL and SIDE[e - OUT_LAG][1] % 2 == 1):
                        output(c - 1, 1 - parity, SIDE[e - OUT_LAG][1])
                    if kind in (FIRST, MIDDLE) and e == ROWS_AT:
                        rows(c + 1, 1 - parity)
                        row_scales(c + 1, 1 - parity)
                    if kind in (FIRST, MIDDLE) and has_job(kind, e - HLOW_LAG) and SIDE[e - HLOW_LAG][0] == "turn":
                        h_low(c + 1, 1 - parity, SIDE[e - HLOW_LAG][1])

            link(pool.memset(ident[:], 0.0))
            pool.affine_select(out=ident[:], in_=ident[:], compare_op=ALU.not_equal, fill=1.0, base=0,
                               pattern=[[-1, P]], channel_multiplier=1).then_inc(ident_done, 2)
            for at, value in ((EPS_AT, EPS), (MINUS_HALF, -0.5), (HALF, 0.5), (G_SCALE_AT, G_SCALE),
                              (MINUS_ONE, -1.0), (ONES, 1.0), (ONES + 1, 1.0)):
                pool.memset(row_const[:, at, :], value)
            pool.memset(decay_c[:], DECAY).then_inc(out_free[0], 1)
            pool.memset(minus_zero_point[:], -ZERO_POINT).then_inc(out_free[1], 1)
            pool.iota(tau_i[:, 0:1], [[1, 1]], base=0, channel_multiplier=1).then_inc(tau_made, 1)
            pool.iota(tau_row[:], [[0, B], [1, TAU]], base=0, channel_multiplier=0).then_inc(tau_made, 1)
            pool.wait_ge(tau_made, 2)
            pool.wait_ge(tau_done, 1)
            pool.tensor_tensor(powers[:, 0:2], decay_c[:], tau_c[:], ALU.pow).then_inc(decay_done, 1)
            rows(0, 0)
            pool.wait_ge(tops_done, 1)
            pool.partition_all_reduce(all_tops[:], tops[:], P, bass.bass_isa.ReduceOp.max).then_inc(all_tops_done, 1)
            pool.memset(q1_sb[:, :, :, 1, :], 0.0).then_inc(q1_low_zero, 1)
            h_low(0, 0, 0)
            row_scales(0, 0)
            h_low(0, 0, 1)
            h_low(0, 0, 2)
            pool.wait_ge(top_q1_done, 1)
            pool.partition_all_reduce(top_q1[:], top_q1_part[:], P, bass.bass_isa.ReduceOp.max
                                      ).then_inc(all_top_q1_done, 1)
            h_low(0, 0, 3)
            pool.wait_ge(q2_quarter, 1)
            pool.partition_all_reduce(first_top_q2[:], q2_quarter_tops[:, 0:1], P, bass.bass_isa.ReduceOp.max
                                      ).then_inc(first_top_q2_done, 1)
            each_chunk(pool, body)


_INS = ["x", "wqkv", "wo", "gate", "m0", "q1", "q2", "s2", "params"]


def kernel(L0_attn_x, L0_attn_Wq, L0_attn_Wk, L0_attn_Wv, L0_attn_Wo, L0_attn_gate, L0_attn_M0,
           L0_ffn_ln_gamma, L0_ffn_ln_beta, L0_ffn_fc1_q, L0_ffn_fc1_scales, L0_ffn_fc1_bias,
           L0_ffn_fc2_q, L0_ffn_fc2_scales, L0_ffn_fc2_bias):
    import concourse.bacc as bacc
    from concourse.bass_utils import run_bass_kernel_spmd

    def blocks(v):
        return np.asarray(v).reshape(-1, P).T

    wq, wk, wv = (np.asarray(w).T.reshape(-1, P, w.shape[0]).transpose(1, 0, 2)
                  for w in (L0_attn_Wq, L0_attn_Wk, L0_attn_Wv))
    values = {
        "x": L0_attn_x, "wqkv": np.concatenate([wq, wk, wv], axis=2), "wo": np.asarray(L0_attn_Wo).T,
        "gate": L0_attn_gate, "m0": np.asarray(L0_attn_M0).T, "q1": L0_ffn_fc1_q, "q2": L0_ffn_fc2_q,
        "s2": L0_ffn_fc2_scales,
        "params": np.concatenate([
            blocks(L0_ffn_ln_gamma), blocks(L0_ffn_ln_beta), blocks(L0_ffn_fc1_bias), blocks(L0_ffn_fc1_scales),
            blocks(L0_ffn_fc2_scales), blocks(L0_ffn_fc2_bias)], axis=1),
    }
    nc = bacc.Bacc("TRN2", target_bir_lowering=False, num_devices=1)
    arrays, args = {}, []
    for name in _INS:
        a = np.ascontiguousarray(values[name])
        arrays[f"in_{name}"] = a
        args.append(nc.dram_tensor(f"in_{name}", a.shape, mybir.dt.from_np(a.dtype), kind="ExternalInput").ap())
    out = nc.dram_tensor("out", L0_attn_x.shape, F32, kind="ExternalOutput").ap()
    build(nc, *args, out)
    return run_bass_kernel_spmd(nc, [arrays], core_ids=[0]).results[0]["out"]
```
